# Optimizing a Trainium2 kernel written in Bass

```python
import numpy as np
import jax
import jax.numpy as jnp

def _softmax(x, axis=-1):
    return jax.nn.softmax(x, axis=axis)

def _gelu(x):
    return jax.nn.gelu(x, approximate=True)

def _silu(x):
    return jax.nn.silu(x)

def _sigmoid(x):
    return jax.nn.sigmoid(x)

def _layernorm(x, axis=-1, eps=1e-05):
    m = jnp.mean(x, axis=axis, keepdims=True)
    v = jnp.var(x, axis=axis, keepdims=True)
    return (x - m) / jnp.sqrt(v + eps)

def _scatter_add(tgt, idx, src, axis=0):
    return tgt.at[idx].add(src)

def _segment_sum(src, seg, n):
    return jax.ops.segment_sum(src, seg, n)
kernel_name = 'mk_gnn_preln_d2_gnn_r32_562cfa'

def setup_inputs(seed: int=0):
    np.random.seed(seed)
    _w = jnp.asarray

    def _rec_inputs():
        import jax
        import jax.numpy as jnp
        _gk = jax.random.key(seed)
        x = -0.0002928 + 1 * jax.random.normal(jax.random.fold_in(_gk, 1), (256, 512), jnp.float32)
        src = jax.random.randint(jax.random.fold_in(_gk, 2), (4096,), 0, 256, jnp.int32)
        dst = jnp.minimum((256 * jax.random.uniform(jax.random.fold_in(_gk, 3), (4096,)) ** 2.0).astype(jnp.int32), 8191)
        _o = jnp.argsort(dst, stable=True)
        src = src[_o]
        dst = dst[_o]
        edge_weight = jax.random.uniform(jax.random.fold_in(_gk, 12), (4096,), jnp.float32, 0.0, 0.999996)
        return (x, src, dst, edge_weight)
    x, src, dst, edge_weight = _rec_inputs()

    def _L0_gnn_setup():
        import jax, jax.numpy as jnp
        import numpy as np
        N, E, D_IN, D_OUT = (256, 8192, 512, 512)
        key = jax.random.key(seed)
        k1, k2, k3 = jax.random.split(key, 3)
        x = jax.random.normal(k1, (N, D_IN), dtype=jnp.float32)
        edge_index = jax.random.randint(k2, (2, E), 0, N, dtype=jnp.int64)
        limit = float(np.sqrt(6.0 / (D_IN + D_OUT)))
        weight = jax.random.uniform(k3, (D_IN, D_OUT), dtype=jnp.float32, minval=-limit, maxval=limit)
        bias = jnp.zeros((D_OUT,), dtype=jnp.float32)
        return {'x': x, 'edge_index': edge_index, 'weight': weight, 'bias': bias}
    _L0_gnn_all = _L0_gnn_setup()
    _L0_gnn_in = {k: v for k, v in _L0_gnn_all.items() if k in ('weight', 'bias')}
    del _L0_gnn_all

    def _L1_gnn_setup():
        import jax, jax.numpy as jnp
        import numpy as np
        N, E, D, K = (625, 5000, 512, 5)
        key = jax.random.key(seed)
        ks = jax.random.split(key, 8)
        return {'x': jax.random.normal(ks[0], (N, D), dtype=jnp.float32), 'edge_index': jax.random.randint(ks[1], (2, E), 0, N, dtype=jnp.int64), 'edge_weight': jax.random.uniform(ks[2], (E,), dtype=jnp.float32), 'ln_gamma': jnp.ones((D,), jnp.float32), 'ln_beta': jnp.zeros((D,), jnp.float32), 'cheb_W': jax.random.normal(ks[3], (K, D, D), dtype=jnp.float32) / np.sqrt(D), 'cheb_b': jnp.zeros((D,), jnp.float32), 'lin_W': jax.random.normal(ks[4], (D, D), dtype=jnp.float32) / np.sqrt(D), 'lin_b': jnp.zeros((D,), jnp.float32)}
    _L1_gnn_all = _L1_gnn_setup()
    _L1_gnn_in = {k: v for k, v in _L1_gnn_all.items() if k in ('ln_gamma', 'ln_beta', 'cheb_W', 'cheb_b', 'lin_W', 'lin_b')}
    del _L1_gnn_all
    return {'x': x, 'src': src, 'dst': dst, 'edge_weight': edge_weight, 'L0_gnn_weight': _L0_gnn_in['weight'], 'L0_gnn_bias': _L0_gnn_in['bias'], 'L1_gnn_ln_gamma': _L1_gnn_in['ln_gamma'], 'L1_gnn_ln_beta': _L1_gnn_in['ln_beta'], 'L1_gnn_cheb_W': _L1_gnn_in['cheb_W'], 'L1_gnn_cheb_b': _L1_gnn_in['cheb_b'], 'L1_gnn_lin_W': _L1_gnn_in['lin_W'], 'L1_gnn_lin_b': _L1_gnn_in['lin_b']}

def reference(x, src, dst, edge_weight, L0_gnn_weight, L0_gnn_bias, L1_gnn_ln_gamma, L1_gnn_ln_beta, L1_gnn_cheb_W, L1_gnn_cheb_b, L1_gnn_lin_W, L1_gnn_lin_b):
    import jax
    import jax.numpy as jnp

    def _L0_gnn_ref(x, edge_index, weight, bias):
        import jax, jax.numpy as jnp
        import numpy as np
        N, E, D_IN, D_OUT = (256, 8192, 512, 512)
        support = x @ weight
        n = x.shape[0]
        adj = jnp.zeros((n, n), dtype=x.dtype).at[edge_index[0], edge_index[1]].set(1.0)
        adj = adj + jnp.eye(n, dtype=x.dtype)
        degree = adj.sum(axis=1, keepdims=True)
        d_inv_sqrt = jnp.where(degree > 0, jax.lax.rsqrt(degree), 0.0)
        adj_normalized = d_inv_sqrt * adj * d_inv_sqrt.T
        out = adj_normalized @ support + bias
        return out

    def _L1_gnn_ref(x, edge_index, edge_weight, ln_gamma, ln_beta, cheb_W, cheb_b, lin_W, lin_b):
        import jax, jax.numpy as jnp
        import numpy as np
        N, E, D, K = (625, 5000, 512, 5)
        n = x.shape[0]
        mu = jnp.mean(x, axis=-1, keepdims=True)
        var = jnp.mean((x - mu) ** 2, axis=-1, keepdims=True)
        xn = (x - mu) * jax.lax.rsqrt(var + 1e-05) * ln_gamma + ln_beta
        row, col = (edge_index[0], edge_index[1])
        deg = jax.ops.segment_sum(edge_weight, row, num_segments=n)
        dinv = jnp.where(deg > 0, jax.lax.rsqrt(jnp.where(deg > 0, deg, 1.0)), 0.0)
        norm_w = -dinv[row] * edge_weight * dinv[col]

        def prop(h):
            return jax.ops.segment_sum(norm_w[:, None] * h[row], col, num_segments=n)
        Tx0 = xn
        out = jnp.einsum('nd,fd->nf', Tx0, cheb_W[0])
        Tx1 = prop(Tx0)
        out = out + jnp.einsum('nd,fd->nf', Tx1, cheb_W[1])
        for k in range(2, cheb_W.shape[0]):
            Tx2 = 2.0 * prop(Tx1) - Tx0
            out = out + jnp.einsum('nd,fd->nf', Tx2, cheb_W[k])
            Tx0, Tx1 = (Tx1, Tx2)
        out = out + cheb_b
        x_graph = jnp.where(out >= 0, out, 0.01 * out)
        return xn @ lin_W.T + lin_b + x_graph
    edge_index = jnp.stack([src, dst])
    h = jnp.maximum(_layernorm(x, axis=-1), 0.0)
    x = x + _L0_gnn_ref(h, edge_index, L0_gnn_weight, L0_gnn_bias)
    h = jnp.maximum(_layernorm(x, axis=-1), 0.0)
    x = x + _L1_gnn_ref(h, edge_index, edge_weight, L1_gnn_ln_gamma, L1_gnn_ln_beta, L1_gnn_cheb_W, L1_gnn_cheb_b, L1_gnn_lin_W, L1_gnn_lin_b)
    return x

_drawn_inputs = setup_inputs


def setup_inputs(seed=0):
    import zlib

    import numpy as np

    out = dict(_drawn_inputs(seed))
    spreads = {'L0_gnn_bias': (0.0, 0.1),
     'L1_gnn_ln_gamma': (1.0, 0.2),
     'L1_gnn_ln_beta': (0.0, 0.1),
     'L1_gnn_cheb_b': (0.0, 0.1),
     'L1_gnn_lin_b': (0.0, 0.1)}
    factors = {}
    for name, (base, spread) in spreads.items():
        noise = np.random.default_rng([zlib.crc32(name.encode()), seed]).standard_normal(out[name].shape)
        drawn = base * np.exp(spread * noise) if base else spread * noise
        out[name] = jnp.asarray(drawn.astype(out[name].dtype))
    for name, factor in factors.items():
        out[name] = (out[name] * factor).astype(out[name].dtype)
    return out
```

```python
from contextlib import ExitStack

import numpy as np

import concourse.bass as bass
import concourse.mybir as mybir

F32 = mybir.dt.float32
F32R = mybir.dt.float32r
BF16 = mybir.dt.bfloat16
I32 = mybir.dt.int32
ALU = mybir.AluOpType
ACT = mybir.ActivationFunctionType

P = 128
N = 256
NH = N // P
E = 4096
EC = E // P
D = 512
DC = D // P
K = 5
EPS = 1e-5
GRP = 4
SR = 2 * GRP

NW = 1 + K + 1
LIN = NW - 1
W_SLOT = [0, 1, 0, 2, 1, 3, 0]
RAW = 2
PIECE = 2
PC = DC // PIECE


def pieces_by(engine):
    pool = {(0, 0), (0, 1), (1, 0), (1, 1)}
    out = [(s, p) for s in range(NW) for p in range(PIECE)]
    return [x for x in out if (x in pool) == (engine == "pool")]


def low_count(s, engine):
    return sum(1 for x in pieces_by(engine) if x[0] <= s)


def build(nc, x, edges, edge_w, w0, wt, cols, rows, out):
    ctx = ExitStack()
    with ctx:
        def sb(name, shape, dt, where=ctx):
            return where.enter_context(nc.sbuf_tensor(name, shape, dt))

        def sem(name):
            return ctx.enter_context(nc.semaphore(name))

        x_sb = sb("x_sb", [P, NH, D], F32)
        x1 = sb("x1", [P, NH, D], F32)
        u = sb("u", [P, NH, D], F32)
        row_bias = sb("row_bias", [P, 3, D], F32)
        col_gb = sb("col_gb", [P, 2, DC], F32)
        t32 = sb("t32", [P, DC, N], F32)
        t_hi = sb("t_hi", [P, DC, N], F32R)
        t_lo = sb("t_lo", [P, DC, N], F32R)
        raw = sb("raw", [P, RAW, DC, D], F32)
        w_hi = [sb(f"w_hi{i}", [P, DC, D], F32R) for i in range(2)]
        w_lo = [sb(f"w_lo{i}", [P, DC, D], F32R) for i in range(2)]
        sup_hi = sb("sup_hi", [P, NH, D], F32R)
        sup_lo = sb("sup_lo", [P, NH, D], F32R)
        adj = sb("adj", [P, NH, N], F32R)
        iota_i = sb("iota_i", [P, N], I32)
        iota = sb("iota", [P, N], BF16)
        eye = sb("eye", [P, P + N], F32)
        ones = sb("ones", [P, P], F32)
        ones_r = sb("ones_r", [P, 2], F32R)
        half_neg = sb("half_neg", [P, NH], F32)
        ed_i = sb("ed_i", [P, 2, EC], I32)
        ed_f = sb("ed_f", [P, 2, EC], F32)
        ew = sb("ew", [P, EC], F32)
        ew_hi = sb("ew_hi", [P, EC], F32R)
        ew_lo = sb("ew_lo", [P, EC], F32)
        stats = sb("stats", [P, 3, NH, 6], F32)
        mv = sb("mv", [P, 3, NH, 2], F32)
        ve = sb("ve", [P, 2, NH], F32)
        rs = sb("rs", [P, 2, NH], F32)
        eps1 = sb("eps1", [P, NH], F32)
        deg0 = sb("deg0", [P, NH], F32)
        dn = sb("dn", [P, NH], F32)
        sup_scale = sb("sup_scale", [P, NH], F32)
        degw = sb("degw", [P, NH], F32)
        deg_not = sb("deg_not", [P, NH], F32)
        deg_safe = sb("deg_safe", [P, NH], F32)
        dpow = sb("dpow", [P, NH], F32)
        dinv = sb("dinv", [P, NH], F32)
        dinv_m2 = sb("dinv_m2", [P, NH], F32)

        edge_mem = ExitStack()
        onehot = sb("onehot", [P, EC, 2, N], BF16, edge_mem)
        wdst = sb("wdst", [P, EC, 2, N], F32R, edge_mem)
        src_r = sb("src_r", [P, SR, N], F32R, edge_mem)
        edge_mem.close()
        w_hi += [sb(f"w_hi{i}", [P, DC, D], F32R) for i in (2, 3)]
        w_lo += [sb(f"w_lo{i}", [P, DC, D], F32R) for i in (2, 3)]
        a_lo = sb("a_lo", [P, NH, N], F32)
        aw = sb("aw", [P, NH, N], F32)
        diag = sb("diag", [P, NH, P], F32)
        p32 = sb("p32", [P, NH, N], F32)
        p_hi = sb("p_hi", [P, NH, N], F32R)
        p_lo = sb("p_lo", [P, NH, N], F32R)
        b32 = sb("b32", [P, K, NH, D], F32)
        b_hi = [sb(f"b_hi{i}", [P, NH, D], F32R) for i in range(2)]
        b_lo = [sb(f"b_lo{i}", [P, NH, D], F32R) for i in range(2)]
        act_out = sb("act_out", [P, NH, D], F32)
        res = sb("res", [P, NH, D], F32)

        bank = [ctx.enter_context(nc.psum_tensor(f"bank{i}", [P, D], F32)) for i in range(8)]
        pair_a, pair_b, pair_c, pair_d = (bank[2 * i:2 * i + 2] for i in range(4))
        count_ps, agg_ps = pair_a, pair_a
        t_ps = pair_b
        sup_ps, aw_ps = pair_c, pair_c
        deg_ps, bc_ps = pair_d[0], pair_d[1]
        z_ps = {4: pair_a, 3: pair_b, 2: pair_d, 1: pair_c, 0: pair_a}
        lin_ps = pair_b

        in_edges, in_ew, in_x, in_cols, in_rows = (sem(n) for n in (
            "in_edges", "in_ew", "in_x", "in_cols", "in_rows"))
        in_w = [sem(f"in_w{i}") for i in range(RAW)]
        out_done = sem("out_done")
        iota_made, iota_cast, eye_clear, eye_made, ones_made, onesr_made, half_made = (sem(n) for n in (
            "iota_made", "iota_cast", "eye_clear", "eye_made", "ones_made", "onesr_made", "half_made"))
        edges_cast, ew_hi_made, ew_ready = sem("edges_cast"), sem("ew_hi_made"), sem("ew_ready")
        onehots = sem("onehots")
        wdsts = sem("wdsts")
        srcs = sem("srcs")
        srcs_used = sem("srcs_used")
        stats_made, mv_made, u_made, ve_made, rs_made, eps1_made = (sem(n) for n in (
            "stats_made", "mv_made", "u_made", "ve_made", "rs_made", "eps1_made"))
        xb_made = sem("xb_made")
        u1_made = sem("u1_made")
        whi_made, wlo_dve, wlo_pool = sem("whi_made"), sem("wlo_dve"), sem("wlo_pool")
        turned, thi_made, tlo_made = sem("turned"), sem("thi_made"), sem("tlo_made")
        counted, adj_made, deg_done, deg_copied, dn_made, sscale_made = (sem(n) for n in (
            "counted", "adj_made", "deg_done", "deg_copied", "dn_made", "sscale_made"))
        sup_done, suphi_made, suplo_made, agg_done, x1_made, x1b_made = (sem(n) for n in (
            "sup_done", "suphi_made", "suplo_made", "agg_done", "x1_made", "x1b_made"))
        xn_made, xturned, t32_made, xhi_made, xlo_made = (sem(n) for n in (
            "xn_made", "xturned", "t32_made", "xhi_made", "xlo_made"))
        aw_done, alo_made, aw_made, guard1, guard2, dpow_made, dinv_made, dinv2_made = (sem(n) for n in (
            "aw_done", "alo_made", "aw_made", "guard1", "guard2", "dpow_made", "dinv_made", "dinv2_made"))
        diag_made, bc_done, p32_made, phi_made, plo_made = (sem(n) for n in (
            "diag_made", "bc_done", "p32_made", "phi_made", "plo_made"))
        z_done = sem("z_done")
        y_done = sem("y_done")
        b32_made, bhi_made, blo_made = sem("b32_made"), sem("bhi_made"), sem("blo_made")
        b2c_made, lin_done, xl_made, g_made, leaky_made, res_made = (sem(n) for n in (
            "b2c_made", "lin_done", "xl_made", "g_made", "leaky_made", "res_made"))

        block = ctx.enter_context(nc.Block())

        @block.sync
        def _(sp):
            sp.dma_start(x_sb[:], x.rearrange("(h p) d -> p h d", p=P)).then_inc(in_x, 16)
            for s in range(NW):
                src = w0 if s == 0 else wt[s - 1]
                if s >= RAW:
                    sp.wait_ge(whi_made, PIECE * (s - RAW + 1))
                    if low_count(s - RAW, "pool"):
                        sp.wait_ge(wlo_pool, low_count(s - RAW, "pool"))
                    if low_count(s - RAW, "dve"):
                        sp.wait_ge(wlo_dve, low_count(s - RAW, "dve"))
                sp.dma_start(raw[:, s % RAW], src.rearrange("(c p) f -> p c f", p=P)).then_inc(in_w[s % RAW], 16)
                if s == 0:
                    sp.dma_start(row_bias[:], rows).then_inc(in_rows, 16)
                    sp.dma_start(col_gb[:], cols).then_inc(in_cols, 16)
            for h in range(NH):
                sp.wait_ge(res_made, h + 1)
                sp.dma_start(out[h * P:(h + 1) * P, :], res[:, h]).then_inc(out_done, 16)
            sp.wait_ge(out_done, 16 * NH)

        @block.gpsimd
        def _(pool):
            nc.gpsimd.iota(iota_i[:], pattern=[[1, N]], base=0, channel_multiplier=0).then_inc(iota_made, 1)
            nc.gpsimd.memset(eye[:], 0.0).then_inc(eye_clear, 1)
            nc.gpsimd.memset(half_neg[:], -0.5).then_inc(half_made, 1)
            pool.wait_ge(eye_clear, 1)
            nc.gpsimd.affine_select(out=eye[:], in_=eye[:], compare_op=ALU.not_equal, fill=1.0, base=P,
                                    pattern=[[-1, P + N]], channel_multiplier=1).then_inc(eye_made, 1)
            nc.gpsimd.memset(ones[:], 1.0).then_inc(ones_made, 1)

            def low(n):
                s, p = pieces_by("pool")[n]
                part = slice(p * PC, (p + 1) * PC)
                slot = W_SLOT[s]
                pool.wait_ge(whi_made, PIECE * s + p + 1)
                if s == 2:
                    pool.wait_ge(sup_done, NH)
                nc.gpsimd.tensor_tensor(w_lo[slot][:, part], raw[:, s % RAW, part],
                                        w_hi[slot][:, part].bitcast(F32), ALU.subtract).then_inc(wlo_pool, 1)

            pool.wait_ge(half_made, 1)
            pool.wait_ge(ve_made, 1)
            nc.gpsimd.tensor_tensor(rs[:, 0], ve[:, 0], half_neg[:], ALU.pow).then_inc(rs_made, 1)
            low(0)
            low(1)
            pool.wait_ge(in_rows, 16)
            pool.wait_ge(u_made, NH)
            for h in range(NH):
                nc.gpsimd.tensor_tensor(x_sb[:, h], x_sb[:, h], row_bias[:, 0], ALU.add).then_inc(xb_made, 1)
            pool.wait_ge(deg_copied, 1)
            nc.gpsimd.tensor_tensor(dn[:], deg0[:], half_neg[:], ALU.pow).then_inc(dn_made, 1)
            pool.wait_ge(rs_made, 1)
            pool.wait_ge(dn_made, 1)
            nc.gpsimd.tensor_tensor(sup_scale[:], dn[:], rs[:, 0], ALU.mult).then_inc(sscale_made, 1)
            low(2)
            low(3)
            for h in range(NH):
                pool.wait_ge(ve_made, 2 + h)
                nc.gpsimd.tensor_tensor(rs[:, 1, h:h + 1], ve[:, 1, h:h + 1], half_neg[:, 0:1],
                                        ALU.pow).then_inc(rs_made, 1)
            for h in range(NH):
                pool.wait_ge(u1_made, h + 1)
                nc.gpsimd.tensor_tensor(x1[:, h], x1[:, h], row_bias[:, 2], ALU.add).then_inc(x1b_made, 1)
            pool.wait_ge(guard2, 1)
            nc.gpsimd.tensor_tensor(dpow[:], deg_safe[:], half_neg[:], ALU.pow).then_inc(dpow_made, 1)
            for h in range(NH):
                pool.wait_ge(b32_made, 2 * NH + h + 1)
                nc.gpsimd.tensor_tensor(b32[:, 0, h], b32[:, 2, h], row_bias[:, 1],
                                        ALU.subtract).then_inc(b2c_made, 1)

        @block.scalar
        def _(act):
            act.dma_start(ed_i[:], edges).then_inc(in_edges, 16)
            act.dma_start(ew[:], edge_w).then_inc(in_ew, 16)

            def high(s):
                slot = W_SLOT[s]
                act.wait_ge(in_w[s % RAW], 16 * (s // RAW + 1))
                if s == 2:
                    act.wait_ge(sup_done, NH)
                elif slot >= 2:
                    act.wait_ge(aw_done, NH)
                elif s == 4:
                    act.wait_ge(y_done, NH)
                elif s == 6:
                    act.wait_ge(z_done, 1)
                for p in range(PIECE):
                    part = slice(p * PC, (p + 1) * PC)
                    nc.scalar.activation(w_hi[slot][:, part], raw[:, s % RAW, part], ACT.Copy).then_inc(whi_made, 1)

            def src_group(g):
                act.wait_ge(onehots, GRP * (g + 1))
                if g >= 2:
                    act.wait_ge(srcs_used, g - 1)
                nc.scalar.activation(src_r[:, (g % 2) * GRP:(g % 2 + 1) * GRP],
                                     onehot[:, g * GRP:(g + 1) * GRP, 0], ACT.Copy).then_inc(srcs, 1)

            high(0)
            for i in range(2):
                act.wait_ge(turned, NH)
                nc.scalar.activation(t_hi[:, 2 * i:2 * i + 2], t_ps[i][:].rearrange("p (c n) -> p c n", c=2),
                                     ACT.Copy).then_inc(thi_made, 1)
            src_group(0)
            src_group(1)
            for h in range(NH):
                act.wait_ge(sscale_made, 1)
                act.wait_ge(sup_done, h + 1)
                nc.scalar.activation(sup_hi[:, h], sup_ps[h][:], ACT.Copy,
                                     scale=sup_scale[:, h:h + 1]).then_inc(suphi_made, 1)
            high(1)
            for g in range(2, EC // GRP):
                src_group(g)
            act.wait_ge(in_cols, 16)
            act.wait_ge(xturned, NH)
            for c in range(DC):
                nc.scalar.activation(t32[:, c], t_ps[c // 2][:, (c % 2) * N:(c % 2 + 1) * N], ACT.Identity,
                                     scale=col_gb[:, 0, c:c + 1], bias=col_gb[:, 1, c:c + 1]).then_inc(t32_made, 1)
            for h in range(NH):
                act.wait_ge(aw_done, h + 1)
                nc.scalar.activation(a_lo[:, h], aw_ps[h][:, N:2 * N], ACT.Copy).then_inc(alo_made, 1)
            high(2)
            act.wait_ge(p32_made, NH)
            nc.scalar.activation(p_hi[:], p32[:], ACT.Copy).then_inc(phi_made, 1)
            high(3)

            def b_copy(i, k):
                for h in range(NH):
                    act.wait_ge(y_done, NH * i + h + 1)
                    nc.scalar.activation(b32[:, k, h], z_ps[k][h][:], ACT.Copy).then_inc(b32_made, 1)

            b_copy(0, 4)
            high(4)
            b_copy(1, 3)
            high(5)
            high(6)

        @block.vector
        def _(dve):
            nc.vector.memset(ones_r[:].bitcast(F32), 1.0).then_inc(onesr_made, 1)
            dve.wait_ge(iota_made, 1)
            nc.vector.tensor_copy(iota[:], iota_i[:]).then_inc(iota_cast, 1)
            dve.wait_ge(in_edges, 16)
            nc.vector.tensor_copy(ed_f[:], ed_i[:]).then_inc(edges_cast, 1)
            dve.wait_ge(in_ew, 16)
            nc.vector.tensor_copy(ew_hi[:], ew[:]).then_inc(ew_hi_made, 1)
            dve.wait_ge(ew_hi_made, 1)
            nc.vector.tensor_tensor(ew_lo[:], ew[:], ew_hi[:].bitcast(F32), ALU.subtract).then_inc(ew_ready, 1)
            dve.wait_ge(edges_cast, 1)
            dve.wait_ge(iota_cast, 1)

            def onehot_loop(first, last):
                with dve.Fori(first // GRP, last // GRP) as g:
                    for j in range(GRP):
                        for side in (0, 1):
                            made = nc.vector.tensor_scalar(onehot[:, g * GRP + j, side], iota[:],
                                                           ed_f[:, side, bass.ds(g * GRP + j, 1)], None,
                                                           ALU.is_equal)
                        made.then_inc(onehots, 1)

            def wdst_loop(first, last):
                with dve.Fori(first // GRP, last // GRP) as g:
                    for j in range(GRP):
                        for part, scale in ((0, ew_hi[:].bitcast(F32)), (1, ew_lo[:])):
                            made = nc.vector.tensor_scalar(wdst[:, g * GRP + j, part], iota[:],
                                                           ed_f[:, 1, bass.ds(g * GRP + j, 1)],
                                                           scale[:, bass.ds(g * GRP + j, 1)],
                                                           ALU.is_equal, ALU.mult)
                        made.then_inc(wdsts, 1)

            def low(n):
                s, p = pieces_by("dve")[n]
                part = slice(p * PC, (p + 1) * PC)
                slot = W_SLOT[s]
                dve.wait_ge(whi_made, PIECE * s + p + 1)
                nc.vector.tensor_tensor(w_lo[slot][:, part], raw[:, s % RAW, part],
                                        w_hi[slot][:, part].bitcast(F32), ALU.subtract).then_inc(wlo_dve, 1)

            onehot_loop(0, EC // 2)

            dve.wait_ge(in_x, 16)
            for h in range(NH):
                nc.vector.bn_stats(stats[:, 0, h], x_sb[:, h]).then_inc(stats_made, 1)
            for h in range(NH):
                dve.wait_ge(stats_made, h + 1)
                nc.vector.bn_aggr(mv[:, 0, h], stats[:, 0, h]).then_inc(mv_made, 1)
            for h in range(NH):
                dve.wait_ge(mv_made, h + 1)
                nc.vector.tensor_scalar(u[:, h], x_sb[:, h], mv[:, 0, h, 0:1], 0.0,
                                        ALU.subtract, ALU.max).then_inc(u_made, 1)
            nc.vector.tensor_scalar(ve[:, 0], mv[:, 0, :, 1], EPS, None, ALU.add).then_inc(ve_made, 1)

            onehot_loop(EC // 2, EC)

            for i in range(2):
                dve.wait_ge(thi_made, i + 1)
                nc.vector.tensor_tensor(t_lo[:, 2 * i:2 * i + 2], t_ps[i][:].rearrange("p (c n) -> p c n", c=2),
                                        t_hi[:, 2 * i:2 * i + 2].bitcast(F32), ALU.subtract).then_inc(tlo_made, 1)
            dve.wait_ge(eye_made, 1)
            for q in range(NH):
                dve.wait_ge(counted, 1)
                nc.vector.scalar_tensor_tensor(out=adj[:, q], in0=count_ps[q][:, 0:N], scalar=1.0,
                                               in1=eye[:, P - q * P:P - q * P + N], op0=ALU.min,
                                               op1=ALU.add).then_inc(adj_made, 1)
            dve.wait_ge(ew_ready, 1)
            wdst_loop(0, 4)
            dve.wait_ge(deg_done, 1)
            nc.vector.tensor_copy(deg0[:], deg_ps[:, 0:2 * NH].rearrange("p (h t) -> p h t", t=2)[:, :, 0])\
                .then_inc(deg_copied, 1)
            wdst_loop(4, 12)
            for h in range(NH):
                dve.wait_ge(suphi_made, h + 1)
                nc.vector.scalar_tensor_tensor(out=sup_lo[:, h], in0=sup_ps[h][:], scalar=sup_scale[:, h:h + 1],
                                               in1=sup_hi[:, h].bitcast(F32), op0=ALU.mult,
                                               op1=ALU.subtract).then_inc(suplo_made, 1)
            wdst_loop(12, 16)

            for h in range(NH):
                dve.wait_ge(agg_done, h + 1)
                dve.wait_ge(dn_made, 1)
                dve.wait_ge(xb_made, h + 1)
                nc.vector.scalar_tensor_tensor(out=x1[:, h], in0=agg_ps[h][:], scalar=dn[:, h:h + 1],
                                               in1=x_sb[:, h], op0=ALU.mult, op1=ALU.add).then_inc(x1_made, 1)
                dve.wait_ge(x1_made, h + 1)
                nc.vector.bn_stats(stats[:, 1, h], x1[:, h]).then_inc(stats_made, 1)
                dve.wait_ge(stats_made, NH + 2 * h + 1)
                nc.vector.bn_aggr(mv[:, 1, h], stats[:, 1, h]).then_inc(mv_made, 1)
                dve.wait_ge(mv_made, NH + 2 * h + 1)
                nc.vector.tensor_scalar(u[:, h], x1[:, h], mv[:, 1, h, 0:1], 0.0,
                                        ALU.subtract, ALU.max).then_inc(u1_made, 1)
                nc.vector.tensor_scalar(eps1[:, h:h + 1], mv[:, 1, h, 1:2], EPS, EPS,
                                        ALU.add, ALU.mult).then_inc(eps1_made, 1)
                dve.wait_ge(u1_made, h + 1)
                nc.vector.bn_stats(stats[:, 2, h], u[:, h]).then_inc(stats_made, 1)
                dve.wait_ge(stats_made, NH + 2 * h + 2)
                nc.vector.bn_aggr(mv[:, 2, h], stats[:, 2, h]).then_inc(mv_made, 1)
                dve.wait_ge(mv_made, NH + 2 * h + 2)
                dve.wait_ge(eps1_made, h + 1)
                nc.vector.tensor_scalar(ve[:, 1, h:h + 1], mv[:, 2, h, 1:2], eps1[:, h:h + 1], None,
                                        ALU.add).then_inc(ve_made, 1)
            for h in range(NH):
                dve.wait_ge(rs_made, 2 + h)
                nc.vector.tensor_scalar(u[:, h], u[:, h], mv[:, 2, h, 0:1], rs[:, 1, h:h + 1],
                                        ALU.subtract, ALU.mult).then_inc(xn_made, 1)
            wdst_loop(16, EC)
            for c in range(0, DC, 2):
                dve.wait_ge(t32_made, c + 2)
                if c == 0:
                    dve.wait_ge(sup_done, NH)
                nc.vector.tensor_copy(t_hi[:, c:c + 2], t32[:, c:c + 2]).then_inc(xhi_made, 1)
                dve.wait_ge(xhi_made, c // 2 + 1)
                nc.vector.tensor_tensor(t_lo[:, c:c + 2], t32[:, c:c + 2], t_hi[:, c:c + 2].bitcast(F32),
                                        ALU.subtract).then_inc(xlo_made, 1)

            for h in range(NH):
                dve.wait_ge(alo_made, h + 1)
                nc.vector.scalar_tensor_tensor(out=aw[:, h], in0=aw_ps[h][:, 0:N], scalar=1.0, in1=a_lo[:, h],
                                               op0=ALU.mult, op1=ALU.add,
                                               accum_out=degw[:, h:h + 1]).then_inc(aw_made, 1)
            dve.wait_ge(aw_made, NH)
            nc.vector.tensor_scalar(deg_not[:], degw[:], 0.0, None, ALU.is_le).then_inc(guard1, 1)
            dve.wait_ge(guard1, 1)
            nc.vector.scalar_tensor_tensor(out=deg_safe[:], in0=degw[:], scalar=0.0, in1=deg_not[:],
                                           op0=ALU.max, op1=ALU.add).then_inc(guard2, 1)
            dve.wait_ge(dpow_made, 1)
            nc.vector.scalar_tensor_tensor(out=dinv[:], in0=degw[:], scalar=0.0, in1=dpow[:],
                                           op0=ALU.is_gt, op1=ALU.mult).then_inc(dinv_made, 1)
            dve.wait_ge(dinv_made, 1)
            nc.vector.tensor_scalar(dinv_m2[:], dinv[:], -2.0, None, ALU.mult).then_inc(dinv2_made, 1)
            for h in range(NH):
                nc.vector.tensor_scalar(diag[:, h], eye[:, P:2 * P], dinv[:, h:h + 1], None,
                                        ALU.mult).then_inc(diag_made, 1)
            low(0)
            low(1)
            dve.wait_ge(dinv2_made, 1)
            dve.wait_ge(bc_done, 1)
            for h in range(NH):
                nc.vector.scalar_tensor_tensor(out=p32[:, h], in0=aw[:, h], scalar=dinv_m2[:, h:h + 1],
                                               in1=bc_ps[:, 0:N], op0=ALU.mult, op1=ALU.mult).then_inc(p32_made, 1)
            dve.wait_ge(phi_made, 1)
            nc.vector.tensor_tensor(p_lo[:], p32[:], p_hi[:].bitcast(F32), ALU.subtract).then_inc(plo_made, 1)

            def b_split(i, k):
                hi, lo = b_hi[i % 2], b_lo[i % 2]
                if k < 3:
                    for h in range(NH):
                        dve.wait_ge(y_done, NH * i + h + 1)
                        nc.vector.tensor_tensor(b32[:, k, h], z_ps[k][h][:], b32[:, k + 2, h],
                                                ALU.subtract).then_inc(b32_made, 1)
                scale = 0.5 if k == 1 else 1.0
                for h in range(NH):
                    dve.wait_ge(b32_made, NH * i + h + 1)
                    nc.vector.tensor_scalar(hi[:, h], b32[:, k, h], scale, None, ALU.mult).then_inc(bhi_made, 1)
                for h in range(NH):
                    dve.wait_ge(bhi_made, NH * i + h + 1)
                    nc.vector.scalar_tensor_tensor(out=lo[:, h], in0=b32[:, k, h], scalar=scale,
                                                   in1=hi[:, h].bitcast(F32), op0=ALU.mult,
                                                   op1=ALU.subtract).then_inc(blo_made, 1)

            b_split(0, 4)
            low(2)
            low(3)
            b_split(1, 3)
            low(4)
            low(5)
            low(6)
            low(7)
            b_split(2, 2)
            low(8)
            low(9)
            b_split(3, 1)
            xl = b32[:, 4]
            for h in range(NH):
                dve.wait_ge(lin_done, h + 1)
                dve.wait_ge(x1b_made, h + 1)
                nc.vector.tensor_tensor(xl[:, h], lin_ps[h][:], x1[:, h], ALU.add).then_inc(xl_made, 1)
            for h in range(NH):
                dve.wait_ge(y_done, NH * 4 + h + 1)
                dve.wait_ge(b2c_made, h + 1)
                nc.vector.tensor_tensor(act_out[:, h], z_ps[0][h][:], b32[:, 0, h],
                                        ALU.subtract).then_inc(g_made, 1)
                dve.wait_ge(g_made, h + 1)
                nc.vector.scalar_tensor_tensor(out=act_out[:, h], in0=act_out[:, h], scalar=0.01,
                                               in1=act_out[:, h], op0=ALU.mult, op1=ALU.max).then_inc(leaky_made, 1)
                dve.wait_ge(leaky_made, h + 1)
                dve.wait_ge(xl_made, h + 1)
                nc.vector.tensor_tensor(res[:, h], act_out[:, h], xl[:, h], ALU.add).then_inc(res_made, 1)

        @block.tensor
        def _(pe):
            def count_chunk(c, first, last):
                for q in range(NH):
                    mm = nc.tensor.matmul(count_ps[q][:, 0:N], onehot[:, c, 1, q * P:(q + 1) * P],
                                          onehot[:, c, 0], start=first, stop=last)
                return mm

            def count_group(g, first=False, last=False):
                for j in range(GRP):
                    pe.wait_ge(onehots, g * GRP + j + 1)
                    mm = count_chunk(g * GRP + j, first and j == 0, last and j == GRP - 1)
                return mm

            count_group(0, first=True)
            with pe.Fori(1, EC // GRP // 2) as g:
                count_group(g)
            pe.wait_ge(eye_made, 1)
            for h in range(NH):
                pe.wait_ge(u_made, h + 1)
                for c in range(DC):
                    mm = nc.tensor.transpose(t_ps[c // 2][:, (c % 2) * N + h * P:(c % 2) * N + (h + 1) * P],
                                             u[:, h, c * P:(c + 1) * P], eye[:, P:2 * P])
                mm.then_inc(turned, 1)
            with pe.Fori(EC // GRP // 2, EC // GRP - 1) as g:
                count_group(g)
            count_group(EC // GRP - 1, last=True).then_inc(counted, 1)

            def low_wait(s):
                if low_count(s, "pool"):
                    pe.wait_ge(wlo_pool, low_count(s, "pool"))
                if low_count(s, "dve"):
                    pe.wait_ge(wlo_dve, low_count(s, "dve"))

            def times_weight(ps, s, h, terms, first, last):
                slot = W_SLOT[s]
                for n, (a, w) in enumerate(terms):
                    for c in range(DC):
                        mm = nc.tensor.matmul(ps[h][:], (t_hi, t_lo)[a][:, c, h * P:(h + 1) * P],
                                              (w_hi, w_lo)[w][slot][:, c],
                                              start=first and n == 0 and c == 0,
                                              stop=last and n == len(terms) - 1 and c == DC - 1)
                return mm

            pe.wait_ge(thi_made, 2)
            pe.wait_ge(whi_made, PIECE)
            for h in range(NH):
                times_weight(sup_ps, 0, h, [(0, 0)], True, False)
            pe.wait_ge(adj_made, NH)
            pe.wait_ge(onesr_made, 1)
            for h in range(NH):
                for q in range(NH):
                    mm = nc.tensor.matmul(deg_ps[:, 2 * h:2 * h + 2], adj[:, q, h * P:(h + 1) * P], ones_r[:],
                                          start=q == 0, stop=q == NH - 1)
            mm.then_inc(deg_done, 1)
            pe.wait_ge(tlo_made, 2)
            for h in range(NH):
                times_weight(sup_ps, 0, h, [(1, 0)], False, False)
            low_wait(0)
            for h in range(NH):
                times_weight(sup_ps, 0, h, [(0, 1)], False, True).then_inc(sup_done, 1)

            for h in range(NH):
                for part, made, tile in ((0, suphi_made, sup_hi), (1, suplo_made, sup_lo)):
                    for q in range(NH):
                        pe.wait_ge(made, q + 1)
                        mm = nc.tensor.matmul(agg_ps[h][:], adj[:, q, h * P:(h + 1) * P], tile[:, q],
                                              start=part == 0 and q == 0, stop=part == 1 and q == NH - 1)
                mm.then_inc(agg_done, 1)

            def weighted(g, first=False, last=False):
                for r in range(2):
                    pe.wait_ge(srcs, 2 * g + r + 1)
                    for j in range(GRP):
                        c = g * SR + r * GRP + j
                        pe.wait_ge(wdsts, c + 1)
                        for m in range(NH):
                            mm = nc.tensor.matmul(aw_ps[m][:], src_r[:, r * GRP + j, m * P:(m + 1) * P],
                                                  wdst[:, c].rearrange("p t n -> p (t n)"),
                                                  start=first and r == 0 and j == 0,
                                                  stop=last and r == 1 and j == GRP - 1)
                            if r == 1 and j == GRP - 1 and last:
                                mm.then_inc(aw_done, 1)
                    if not (last and r == 1):
                        mm.then_inc(srcs_used, 1)

            pe.wait_ge(suplo_made, NH)
            weighted(0, first=True)
            with pe.Fori(1, EC // SR - 1) as g:
                weighted(g)
            weighted(EC // SR - 1, last=True)

            for h in range(NH):
                pe.wait_ge(xn_made, h + 1)
                pe.wait_ge(tlo_made, 2)
                for c in range(DC):
                    mm = nc.tensor.transpose(t_ps[c // 2][:, (c % 2) * N + h * P:(c % 2) * N + (h + 1) * P],
                                             u[:, h, c * P:(c + 1) * P], eye[:, P:2 * P])
                mm.then_inc(xturned, 1)

            def z_term(s, ps, closes):
                pe.wait_ge(whi_made, PIECE * (s + 1))
                for h in range(NH):
                    times_weight(ps, s, h, [(0, 0), (1, 0)], True, False)
                low_wait(s)
                for h in range(NH):
                    mm = times_weight(ps, s, h, [(0, 1)], False, closes is not None)
                    if closes is not None:
                        mm.then_inc(closes, 1)
                    elif h == NH - 1:
                        mm.then_inc(z_done, 1)

            def propagate(i, k):
                hi, lo = b_hi[(i - 1) % 2], b_lo[(i - 1) % 2]
                for h in range(NH):
                    for n, (pt, bt, made) in enumerate(((p_hi, hi, bhi_made), (p_lo, hi, bhi_made),
                                                        (p_hi, lo, blo_made))):
                        for m in range(NH):
                            pe.wait_ge(made, NH * (i - 1) + m + 1)
                            mm = nc.tensor.matmul(z_ps[k][h][:], pt[:, m, h * P:(h + 1) * P], bt[:, m],
                                                  start=False, stop=n == 2 and m == NH - 1)
                    mm.then_inc(y_done, 1)

            pe.wait_ge(xlo_made, 2)
            pe.wait_ge(x1_made, NH)
            z_term(1, z_ps[4], y_done)
            pe.wait_ge(ones_made, 1)
            pe.wait_ge(diag_made, NH)
            pe.wait_ge(deg_copied, 1)
            nc.tensor.matmul(bc_ps[:, 0:N], ones[:], diag[:].rearrange("p h n -> p (h n)"), start=True,
                             stop=True).then_inc(bc_done, 1)
            z_term(2, z_ps[3], None)
            pe.wait_ge(plo_made, 1)
            propagate(1, 3)
            z_term(3, z_ps[2], None)
            propagate(2, 2)
            z_term(4, z_ps[1], None)
            propagate(3, 1)
            z_term(5, z_ps[0], None)
            z_term(6, lin_ps, lin_done)
            propagate(4, 0)


def kernel(x, src, dst, edge_weight, L0_gnn_weight, L0_gnn_bias, L1_gnn_ln_gamma, L1_gnn_ln_beta,
           L1_gnn_cheb_W, L1_gnn_cheb_b, L1_gnn_lin_W, L1_gnn_lin_b):
    import concourse.bacc as bacc
    from concourse.bass_utils import run_bass_kernel_spmd

    a = {k: np.asarray(v) for k, v in locals().items() if k not in ("bacc", "run_bass_kernel_spmd")}
    cheb = a["L1_gnn_cheb_W"]
    arrays = {
        "x": a["x"],
        "edges": np.stack([a["src"].reshape(P, EC), a["dst"].reshape(P, EC)], axis=1),
        "edge_w": a["edge_weight"].reshape(P, EC),
        "w0": a["L0_gnn_weight"],
        "wt": np.stack([cheb[k].T for k in range(K - 1, -1, -1)] + [a["L1_gnn_lin_W"].T]),
        "cols": np.stack([a[n].reshape(DC, P).T for n in ("L1_gnn_ln_gamma", "L1_gnn_ln_beta")], axis=1),
        "rows": np.broadcast_to(np.stack([a["L0_gnn_bias"], a["L1_gnn_cheb_b"], a["L1_gnn_lin_b"]]), (P, 3, D)),
    }
    arrays = {n: np.ascontiguousarray(v) for n, v in arrays.items()}
    nc = bacc.Bacc("TRN2", target_bir_lowering=False, num_devices=1)
    aps = [nc.dram_tensor(n, v.shape, mybir.dt.from_np(v.dtype), kind="ExternalInput").ap()
           for n, v in arrays.items()]
    aps.append(nc.dram_tensor("out", (N, D), F32, kind="ExternalOutput").ap())
    build(nc, *aps)
    return run_bass_kernel_spmd(nc, [arrays], core_ids=[0]).results[0]["out"]
```

```python
from contextlib import ExitStack

import numpy as np

import concourse.bass as bass
import concourse.mybir as mybir

F32 = mybir.dt.float32
F32R = mybir.dt.float32r
BF16 = mybir.dt.bfloat16
I32 = mybir.dt.int32
ALU = mybir.AluOpType
ACT = mybir.ActivationFunctionType

P = 128
N = 256
NH = N // P
E = 4096
EC = E // P
D = 512
DC = D // P
K = 5
EPS = 1e-5
GRP = 8
NG = EC // GRP
LOW_BY_ACT = [2]

NW = 1 + K + 1
LIN = NW - 1
W_SLOT = [0, 1, 0, 2, 1, 3, 0]
RAW = 2
PIECE = 2
PC = DC // PIECE


def pieces_by(engine):
    pool = {(0, 0), (0, 1), (1, 0), (1, 1)}
    out = [(s, p) for s in range(NW) for p in range(PIECE)]
    return [x for x in out if (x in pool) == (engine == "pool")]


def low_count(s, engine):
    return sum(1 for x in pieces_by(engine) if x[0] <= s)


def build(nc, x, edges, edge_w, w0, wt, cols, rows, out):
    ctx = ExitStack()
    with ctx:
        def sb(name, shape, dt, where=ctx):
            return where.enter_context(nc.sbuf_tensor(name, shape, dt))

        def sem(name):
            return ctx.enter_context(nc.semaphore(name))

        x_sb = sb("x_sb", [P, NH, D], F32)
        x1 = sb("x1", [P, NH, D], F32)
        u = sb("u", [P, NH, D], F32)
        row_bias = sb("row_bias", [P, 3, D], F32)
        col_gb = sb("col_gb", [P, 2, DC], F32)
        t32 = sb("t32", [P, DC, N], F32)
        t_hi = sb("t_hi", [P, DC, N], F32R)
        t_lo = sb("t_lo", [P, DC, N], F32R)
        raw = sb("raw", [P, RAW, DC, D], F32)
        w_hi = [sb(f"w_hi{i}", [P, DC, D], F32R) for i in range(2)]
        w_lo = [sb(f"w_lo{i}", [P, DC, D], F32R) for i in range(2)]
        sup_hi = sb("sup_hi", [P, NH, D], F32R)
        sup_lo = sb("sup_lo", [P, NH, D], F32R)
        adj = sb("adj", [P, NH, N], F32R)
        iota_i = sb("iota_i", [P, N], I32)
        iota = sb("iota", [P, N], BF16)
        eye = sb("eye", [P, P + N], F32)
        ones = sb("ones", [P, P], F32)
        ones_r = sb("ones_r", [P, 2], F32R)
        half_neg = sb("half_neg", [P, NH], F32)
        ed_i = sb("ed_i", [P, 2, EC], I32)
        ed_f = sb("ed_f", [P, 2, EC], F32)
        ew = sb("ew", [P, EC], F32)
        ew_hi = sb("ew_hi", [P, EC], F32R)
        ew_lo = sb("ew_lo", [P, EC], F32)
        x_sum = sb("x_sum", [P, NH], F32)
        x_nmean = sb("x_nmean", [P, NH], F32)
        x_sq = sb("x_sq", [P, NH], F32)
        scratch = sb("scratch", [P, D], F32)
        stats = sb("stats", [P, 2, NH, 6], F32)
        mv = sb("mv", [P, 2, NH, 2], F32)
        ve = sb("ve", [P, 2, NH], F32)
        rs = sb("rs", [P, 2, NH], F32)
        eps1 = sb("eps1", [P, NH], F32)
        deg0 = sb("deg0", [P, NH], F32)
        dn = sb("dn", [P, NH], F32)
        sup_scale = sb("sup_scale", [P, NH], F32)
        degw = sb("degw", [P, NH], F32)
        deg_not = sb("deg_not", [P, NH], F32)
        deg_safe = sb("deg_safe", [P, NH], F32)
        dpow = sb("dpow", [P, NH], F32)
        dinv = sb("dinv", [P, NH], F32)
        dinv_m2 = sb("dinv_m2", [P, NH], F32)

        edge_mem = ExitStack()
        onehot = sb("onehot", [P, EC, 2, N], BF16, edge_mem)
        wdst_r = sb("wdst_r", [P, EC, 2, N], F32R, edge_mem)
        src_r = sb("src_r", [P, 2, GRP, N], F32R, edge_mem)
        edge_mem.close()
        w_hi += [sb(f"w_hi{i}", [P, DC, D], F32R) for i in (2, 3)]
        w_lo += [sb(f"w_lo{i}", [P, DC, D], F32R) for i in (2, 3)]
        a_lo = sb("a_lo", [P, NH, N], F32)
        aw = sb("aw", [P, NH, N], F32)
        diag = sb("diag", [P, NH, P], F32)
        p32 = sb("p32", [P, NH, N], F32)
        p_hi = sb("p_hi", [P, NH, N], F32R)
        p_lo = sb("p_lo", [P, NH, N], F32R)
        b32 = sb("b32", [P, K, NH, D], F32)
        b_hi = [sb(f"b_hi{i}", [P, NH, D], F32R) for i in range(2)]
        b_lo = [sb(f"b_lo{i}", [P, NH, D], F32R) for i in range(2)]
        act_out = sb("act_out", [P, NH, D], F32)
        leaky = sb("leaky", [P, NH, D], F32)
        res = sb("res", [P, NH, D], F32)

        bank = [ctx.enter_context(nc.psum_tensor(f"bank{i}", [P, D], F32)) for i in range(8)]
        pair_a, pair_b, pair_c, pair_d = (bank[2 * i:2 * i + 2] for i in range(4))
        count_ps, agg_ps = pair_a, pair_a
        t_ps = pair_b
        sup_ps, aw_ps = pair_c, pair_d
        deg_ps, bc_ps = pair_a[0], pair_c[0]
        z_ps = {4: pair_a, 3: pair_b, 2: pair_d, 1: pair_c, 0: pair_a}
        lin_ps = pair_b

        in_edges, in_ew, in_cols, in_rows = (sem(n) for n in ("in_edges", "in_ew", "in_cols", "in_rows"))
        in_x = [sem(f"in_x{i}") for i in range(NH)]
        in_w = [sem(f"in_w{i}") for i in range(RAW)]
        out_done = sem("out_done")
        iota_made, iota_cast, eye_clear, eye_made, ones_made, onesr_made, half_made = (sem(n) for n in (
            "iota_made", "iota_cast", "eye_clear", "eye_made", "ones_made", "onesr_made", "half_made"))
        edges_cast, ew_hi_made, ew_ready = sem("edges_cast"), sem("ew_hi_made"), sem("ew_ready")
        onehots = sem("onehots")
        wdst_hi, wdst_lo, wdst_lo_act = sem("wdst_hi"), sem("wdst_lo"), sem("wdst_lo_act")
        srcs = sem("srcs")
        srcs_used = sem("srcs_used")
        stats_made, mv_made, u_made, ve_made, rs_made, eps1_made = (sem(n) for n in (
            "stats_made", "mv_made", "u_made", "ve_made", "rs_made", "eps1_made"))
        xb_made = sem("xb_made")
        sum_made, mean_made, sq_made = sem("sum_made"), sem("mean_made"), sem("sq_made")
        u1_made = sem("u1_made")
        whi_made, wlo_dve, wlo_pool = sem("whi_made"), sem("wlo_dve"), sem("wlo_pool")
        turned, thi_made, tlo_made = sem("turned"), sem("thi_made"), sem("tlo_made")
        counted, adj_made, deg_done, deg_copied, dn_made, sscale_made = (sem(n) for n in (
            "counted", "adj_made", "deg_done", "deg_copied", "dn_made", "sscale_made"))
        sup_done, suphi_made, suplo_made, agg_done, x1_made, x1b_made = (sem(n) for n in (
            "sup_done", "suphi_made", "suplo_made", "agg_done", "x1_made", "x1b_made"))
        xn_made, xturned, t32_made, xhi_made, xlo_made = (sem(n) for n in (
            "xn_made", "xturned", "t32_made", "xhi_made", "xlo_made"))
        aw_done, alo_made, aw_made, guard1, guard2, dpow_made, dinv_made, dinv2_made = (sem(n) for n in (
            "aw_done", "alo_made", "aw_made", "guard1", "guard2", "dpow_made", "dinv_made", "dinv2_made"))
        diag_made, bc_done, p32_made, phi_made, plo_made = (sem(n) for n in (
            "diag_made", "bc_done", "p32_made", "phi_made", "plo_made"))
        z_done = sem("z_done")
        y_done = sem("y_done")
        b32_made, bhi_made, blo_made = sem("b32_made"), sem("bhi_made"), sem("blo_made")
        b2c_made, lin_done, xl_made, g_made, leaky_made, res_made = (sem(n) for n in (
            "b2c_made", "lin_done", "xl_made", "g_made", "leaky_made", "res_made"))

        block = ctx.enter_context(nc.Block())

        @block.sync
        def _(sp):
            sp.dma_start(ed_i[:], edges).then_inc(in_edges, 16)
            for h in range(NH):
                sp.dma_start(x_sb[:, h], x[h * P:(h + 1) * P, :]).then_inc(in_x[h], 16)
            sp.dma_start(ew[:], edge_w).then_inc(in_ew, 16)
            for s in range(NW):
                src = w0 if s == 0 else wt[s - 1]
                if s >= RAW:
                    sp.wait_ge(whi_made, PIECE * (s - RAW + 1))
                    if low_count(s - RAW, "pool"):
                        sp.wait_ge(wlo_pool, low_count(s - RAW, "pool"))
                    if low_count(s - RAW, "dve"):
                        sp.wait_ge(wlo_dve, low_count(s - RAW, "dve"))
                sp.dma_start(raw[:, s % RAW], src.rearrange("(c p) f -> p c f", p=P)).then_inc(in_w[s % RAW], 16)
                if s == 0:
                    sp.dma_start(row_bias[:], rows).then_inc(in_rows, 16)
                    sp.dma_start(col_gb[:], cols).then_inc(in_cols, 16)
            for h in range(NH):
                sp.wait_ge(res_made, h + 1)
                sp.dma_start(out[h * P:(h + 1) * P, :], res[:, h]).then_inc(out_done, 16)
            sp.wait_ge(out_done, 16 * NH)

        @block.gpsimd
        def _(pool):
            nc.gpsimd.iota(iota_i[:], pattern=[[1, N]], base=0, channel_multiplier=0).then_inc(iota_made, 1)
            nc.gpsimd.memset(eye[:], 0.0).then_inc(eye_clear, 1)
            nc.gpsimd.memset(half_neg[:], -0.5).then_inc(half_made, 1)
            pool.wait_ge(eye_clear, 1)
            nc.gpsimd.affine_select(out=eye[:], in_=eye[:], compare_op=ALU.not_equal, fill=1.0, base=P,
                                    pattern=[[-1, P + N]], channel_multiplier=1).then_inc(eye_made, 1)
            nc.gpsimd.memset(ones[:], 1.0).then_inc(ones_made, 1)

            def low(n):
                s, p = pieces_by("pool")[n]
                part = slice(p * PC, (p + 1) * PC)
                slot = W_SLOT[s]
                pool.wait_ge(whi_made, PIECE * s + p + 1)
                if s == 2:
                    pool.wait_ge(sup_done, NH)
                nc.gpsimd.tensor_tensor(w_lo[slot][:, part], raw[:, s % RAW, part],
                                        w_hi[slot][:, part].bitcast(F32), ALU.subtract).then_inc(wlo_pool, 1)

            low(0)
            low(1)
            pool.wait_ge(half_made, 1)
            pool.wait_ge(ve_made, 1)
            nc.gpsimd.tensor_tensor(rs[:, 0], ve[:, 0], half_neg[:], ALU.pow).then_inc(rs_made, 1)
            pool.wait_ge(in_rows, 16)
            pool.wait_ge(sq_made, NH)
            for h in range(NH):
                nc.gpsimd.tensor_tensor(x_sb[:, h], x_sb[:, h], row_bias[:, 0], ALU.add).then_inc(xb_made, 1)
            pool.wait_ge(deg_copied, 1)
            nc.gpsimd.tensor_tensor(dn[:], deg0[:], half_neg[:], ALU.pow).then_inc(dn_made, 1)
            pool.wait_ge(rs_made, 1)
            pool.wait_ge(dn_made, 1)
            nc.gpsimd.tensor_tensor(sup_scale[:], dn[:], rs[:, 0], ALU.mult).then_inc(sscale_made, 1)
            low(2)
            low(3)
            pool.wait_ge(ve_made, 2)
            nc.gpsimd.tensor_tensor(rs[:, 1], ve[:, 1], half_neg[:], ALU.pow).then_inc(rs_made, 1)
            for h in range(NH):
                pool.wait_ge(u1_made, h + 1)
                nc.gpsimd.tensor_tensor(x1[:, h], x1[:, h], row_bias[:, 2], ALU.add).then_inc(x1b_made, 1)
            pool.wait_ge(guard2, 1)
            nc.gpsimd.tensor_tensor(dpow[:], deg_safe[:], half_neg[:], ALU.pow).then_inc(dpow_made, 1)
            for h in range(NH):
                pool.wait_ge(b32_made, 2 * NH + h + 1)
                nc.gpsimd.tensor_tensor(b32[:, 0, h], b32[:, 2, h], row_bias[:, 1],
                                        ALU.subtract).then_inc(b2c_made, 1)

        @block.scalar
        def _(act):
            def high(s):
                slot = W_SLOT[s]
                act.wait_ge(in_w[s % RAW], 16 * (s // RAW + 1))
                if s == 2:
                    act.wait_ge(sup_done, NH)
                elif slot >= 2:
                    act.wait_ge(aw_done, NH)
                elif s == 4:
                    act.wait_ge(y_done, NH)
                elif s == 6:
                    act.wait_ge(z_done, 1)
                for p in range(PIECE):
                    part = slice(p * PC, (p + 1) * PC)
                    nc.scalar.activation(w_hi[slot][:, part], raw[:, s % RAW, part], ACT.Copy).then_inc(whi_made, 1)

            def wdst(g, part):
                scale, made = ((ew_hi[:].bitcast(F32), wdst_hi), (ew_lo[:], wdst_lo_act))[part]
                act.wait_ge(ew_ready, 1)
                for c in range(g * GRP, (g + 1) * GRP):
                    act.wait_ge(onehots, c + 1)
                    last = nc.scalar.activation(wdst_r[:, c, part], onehot[:, c, 1], ACT.Copy,
                                                scale=scale[:, c:c + 1])
                    if part == 0:
                        last.then_inc(made, 1)
                if part == 1:
                    last.then_inc(made, 1)

            for h in range(NH):
                act.wait_ge(in_x[h], 16)
                nc.scalar.activation(scratch[:], x_sb[:, h], ACT.Copy, accum_out=x_sum[:, h:h + 1]).then_inc(sum_made, 1)
                act.wait_ge(sum_made, h + 1)
            for h in range(NH):
                act.wait_ge(mean_made, h + 1)
                nc.scalar.activation(u[:, h], x_sb[:, h], ACT.Relu, bias=x_nmean[:, h:h + 1]).then_inc(u_made, 1)
            high(0)
            for h in range(NH):
                nc.scalar.activation(scratch[:], x_sb[:, h], ACT.Square, bias=x_nmean[:, h:h + 1],
                                     accum_out=x_sq[:, h:h + 1]).then_inc(sq_made, 1)
                act.wait_ge(sq_made, h + 1)
            for i in range(2):
                act.wait_ge(turned, NH)
                nc.scalar.activation(t_hi[:, 2 * i:2 * i + 2], t_ps[i][:].rearrange("p (c n) -> p c n", c=2),
                                     ACT.Copy).then_inc(thi_made, 1)
            wdst(0, 0)
            high(1)
            wdst(1, 0)
            for h in range(NH):
                act.wait_ge(sscale_made, 1)
                act.wait_ge(sup_done, h + 1)
                nc.scalar.activation(sup_hi[:, h], sup_ps[h][:], ACT.Copy,
                                     scale=sup_scale[:, h:h + 1]).then_inc(suphi_made, 1)
            wdst(2, 0)
            wdst(2, 1)
            wdst(3, 0)
            act.wait_ge(in_cols, 16)
            act.wait_ge(xturned, NH)
            for c in range(DC):
                nc.scalar.activation(t32[:, c], t_ps[c // 2][:, (c % 2) * N:(c % 2 + 1) * N], ACT.Identity,
                                     scale=col_gb[:, 0, c:c + 1], bias=col_gb[:, 1, c:c + 1]).then_inc(t32_made, 1)
            def b_copy(i, k):
                for h in range(NH):
                    act.wait_ge(y_done, NH * i + h + 1)
                    nc.scalar.activation(b32[:, k, h], z_ps[k][h][:], ACT.Copy).then_inc(b32_made, 1)

            high(2)
            b_copy(0, 4)
            for h in range(NH):
                act.wait_ge(aw_done, h + 1)
                nc.scalar.activation(a_lo[:, h], aw_ps[h][:, N:2 * N], ACT.Copy).then_inc(alo_made, 1)
            high(3)
            act.wait_ge(p32_made, NH)
            nc.scalar.activation(p_hi[:], p32[:], ACT.Copy).then_inc(phi_made, 1)
            high(4)
            b_copy(1, 3)
            high(5)
            high(6)

        @block.vector
        def _(dve):
            nc.vector.memset(ones_r[:].bitcast(F32), 1.0).then_inc(onesr_made, 1)
            dve.wait_ge(iota_made, 1)
            nc.vector.tensor_copy(iota[:], iota_i[:]).then_inc(iota_cast, 1)
            dve.wait_ge(in_edges, 16)
            nc.vector.tensor_copy(ed_f[:], ed_i[:]).then_inc(edges_cast, 1)
            dve.wait_ge(edges_cast, 1)
            dve.wait_ge(iota_cast, 1)

            def onehot_chunks(first, count):
                for j in range(count):
                    for side in (0, 1):
                        made = nc.vector.tensor_scalar(onehot[:, first + j, side], iota[:],
                                                       ed_f[:, side, bass.ds(first + j, 1)], None, ALU.is_equal)
                    made.then_inc(onehots, 1)

            def wdst_low(g):
                chunks = slice(g * GRP, (g + 1) * GRP)
                dve.wait_ge(ew_ready, 1)
                dve.wait_ge(onehots, (g + 1) * GRP)
                nc.vector.tensor_tensor(wdst_r[:, chunks, 1], onehot[:, chunks, 1],
                                        ew_lo[:, chunks].unsqueeze(2).broadcast_to([P, GRP, N]),
                                        ALU.mult).then_inc(wdst_lo, 1)

            def low(n):
                s, p = pieces_by("dve")[n]
                part = slice(p * PC, (p + 1) * PC)
                slot = W_SLOT[s]
                dve.wait_ge(whi_made, PIECE * s + p + 1)
                nc.vector.tensor_tensor(w_lo[slot][:, part], raw[:, s % RAW, part],
                                        w_hi[slot][:, part].bitcast(F32), ALU.subtract).then_inc(wlo_dve, 1)

            def src_group(g):
                dve.wait_ge(onehots, GRP * (g + 1))
                if g >= 2:
                    dve.wait_ge(srcs_used, g - 1)
                nc.vector.tensor_copy(src_r[:, g % 2], onehot[:, g * GRP:(g + 1) * GRP, 0]).then_inc(srcs, 1)

            onehot_chunks(0, GRP)
            dve.wait_ge(in_ew, 16)
            nc.vector.tensor_copy(ew_hi[:], ew[:]).then_inc(ew_hi_made, 1)
            dve.wait_ge(ew_hi_made, 1)
            nc.vector.tensor_tensor(ew_lo[:], ew[:], ew_hi[:].bitcast(F32), ALU.subtract).then_inc(ew_ready, 1)
            for h in range(NH):
                dve.wait_ge(sum_made, h + 1)
                nc.vector.tensor_scalar(x_nmean[:, h:h + 1], x_sum[:, h:h + 1], -1.0 / D, None,
                                        ALU.mult).then_inc(mean_made, 1)
            body = (EC - GRP) // 2
            with dve.Fori(0, 2) as i:
                onehot_chunks(i * body + GRP, body)
            dve.wait_ge(sq_made, NH)
            nc.vector.tensor_scalar(ve[:, 0], x_sq[:], 1.0 / D, EPS, ALU.mult, ALU.add).then_inc(ve_made, 1)
            for i in range(2):
                dve.wait_ge(thi_made, i + 1)
                nc.vector.tensor_tensor(t_lo[:, 2 * i:2 * i + 2], t_ps[i][:].rearrange("p (c n) -> p c n", c=2),
                                        t_hi[:, 2 * i:2 * i + 2].bitcast(F32), ALU.subtract).then_inc(tlo_made, 1)
            src_group(0)
            dve.wait_ge(eye_made, 1)
            for q in range(NH):
                dve.wait_ge(counted, 1)
                nc.vector.scalar_tensor_tensor(out=adj[:, q], in0=count_ps[q][:, 0:N], scalar=1.0,
                                               in1=eye[:, P - q * P:P - q * P + N], op0=ALU.min,
                                               op1=ALU.add).then_inc(adj_made, 1)
            src_group(1)
            dve.wait_ge(deg_done, 1)
            nc.vector.tensor_copy(deg0[:], deg_ps[:, 0:2 * NH].rearrange("p (h t) -> p h t", t=2)[:, :, 0])\
                .then_inc(deg_copied, 1)
            wdst_low(0)
            for h in range(NH):
                dve.wait_ge(suphi_made, h + 1)
                nc.vector.scalar_tensor_tensor(out=sup_lo[:, h], in0=sup_ps[h][:], scalar=sup_scale[:, h:h + 1],
                                               in1=sup_hi[:, h].bitcast(F32), op0=ALU.mult,
                                               op1=ALU.subtract).then_inc(suplo_made, 1)
            wdst_low(1)

            for h in range(NH):
                dve.wait_ge(agg_done, h + 1)
                dve.wait_ge(dn_made, 1)
                dve.wait_ge(xb_made, h + 1)
                nc.vector.scalar_tensor_tensor(out=x1[:, h], in0=agg_ps[h][:], scalar=dn[:, h:h + 1],
                                               in1=x_sb[:, h], op0=ALU.mult, op1=ALU.add).then_inc(x1_made, 1)
            for h in range(NH):
                dve.wait_ge(x1_made, h + 1)
                nc.vector.bn_stats(stats[:, 0, h], x1[:, h]).then_inc(stats_made, 1)
            for h in range(NH):
                dve.wait_ge(stats_made, h + 1)
                nc.vector.bn_aggr(mv[:, 0, h], stats[:, 0, h]).then_inc(mv_made, 1)
            for h in range(NH):
                dve.wait_ge(mv_made, h + 1)
                nc.vector.tensor_scalar(u[:, h], x1[:, h], mv[:, 0, h, 0:1], 0.0,
                                        ALU.subtract, ALU.max).then_inc(u1_made, 1)
            nc.vector.tensor_scalar(eps1[:], mv[:, 0, :, 1], EPS, EPS, ALU.add, ALU.mult).then_inc(eps1_made, 1)
            for h in range(NH):
                dve.wait_ge(u1_made, h + 1)
                nc.vector.bn_stats(stats[:, 1, h], u[:, h]).then_inc(stats_made, 1)
            for h in range(NH):
                dve.wait_ge(stats_made, NH + h + 1)
                nc.vector.bn_aggr(mv[:, 1, h], stats[:, 1, h]).then_inc(mv_made, 1)
            dve.wait_ge(mv_made, 2 * NH)
            dve.wait_ge(eps1_made, 1)
            nc.vector.tensor_tensor(ve[:, 1], mv[:, 1, :, 1], eps1[:], ALU.add).then_inc(ve_made, 1)
            src_group(2)
            for h in range(NH):
                dve.wait_ge(rs_made, 2)
                nc.vector.tensor_scalar(u[:, h], u[:, h], mv[:, 1, h, 0:1], rs[:, 1, h:h + 1],
                                        ALU.subtract, ALU.mult).then_inc(xn_made, 1)
            wdst_low(3)
            src_group(3)
            for c in range(0, DC, 2):
                dve.wait_ge(t32_made, c + 2)
                if c == 0:
                    dve.wait_ge(sup_done, NH)
                nc.vector.tensor_copy(t_hi[:, c:c + 2], t32[:, c:c + 2]).then_inc(xhi_made, 1)
                dve.wait_ge(xhi_made, c // 2 + 1)
                nc.vector.tensor_tensor(t_lo[:, c:c + 2], t32[:, c:c + 2], t_hi[:, c:c + 2].bitcast(F32),
                                        ALU.subtract).then_inc(xlo_made, 1)

            def b_split(i, k):
                hi, lo = b_hi[i % 2], b_lo[i % 2]
                if k < 3:
                    for h in range(NH):
                        dve.wait_ge(y_done, NH * i + h + 1)
                        nc.vector.tensor_tensor(b32[:, k, h], z_ps[k][h][:], b32[:, k + 2, h],
                                                ALU.subtract).then_inc(b32_made, 1)
                scale = 0.5 if k == 1 else 1.0
                for h in range(NH):
                    dve.wait_ge(b32_made, NH * i + h + 1)
                    nc.vector.tensor_scalar(hi[:, h], b32[:, k, h], scale, None, ALU.mult).then_inc(bhi_made, 1)
                for h in range(NH):
                    dve.wait_ge(bhi_made, NH * i + h + 1)
                    nc.vector.scalar_tensor_tensor(out=lo[:, h], in0=b32[:, k, h], scalar=scale,
                                                   in1=hi[:, h].bitcast(F32), op0=ALU.mult,
                                                   op1=ALU.subtract).then_inc(blo_made, 1)

            low(0)
            low(1)
            for h in range(NH):
                dve.wait_ge(alo_made, h + 1)
                nc.vector.scalar_tensor_tensor(out=aw[:, h], in0=aw_ps[h][:, 0:N], scalar=1.0, in1=a_lo[:, h],
                                               op0=ALU.mult, op1=ALU.add,
                                               accum_out=degw[:, h:h + 1]).then_inc(aw_made, 1)
            dve.wait_ge(aw_made, NH)
            nc.vector.tensor_scalar(deg_not[:], degw[:], 0.0, None, ALU.is_le).then_inc(guard1, 1)
            dve.wait_ge(guard1, 1)
            nc.vector.scalar_tensor_tensor(out=deg_safe[:], in0=degw[:], scalar=0.0, in1=deg_not[:],
                                           op0=ALU.max, op1=ALU.add).then_inc(guard2, 1)
            dve.wait_ge(dpow_made, 1)
            nc.vector.scalar_tensor_tensor(out=dinv[:], in0=degw[:], scalar=0.0, in1=dpow[:],
                                           op0=ALU.is_gt, op1=ALU.mult).then_inc(dinv_made, 1)
            dve.wait_ge(dinv_made, 1)
            nc.vector.tensor_scalar(dinv_m2[:], dinv[:], -2.0, None, ALU.mult).then_inc(dinv2_made, 1)
            for h in range(NH):
                nc.vector.tensor_scalar(diag[:, h], eye[:, P:2 * P], dinv[:, h:h + 1], None,
                                        ALU.mult).then_inc(diag_made, 1)
            b_split(0, 4)
            low(2)
            low(3)
            dve.wait_ge(dinv2_made, 1)
            dve.wait_ge(bc_done, 1)
            for h in range(NH):
                nc.vector.scalar_tensor_tensor(out=p32[:, h], in0=aw[:, h], scalar=dinv_m2[:, h:h + 1],
                                               in1=bc_ps[:, 0:N], op0=ALU.mult, op1=ALU.mult).then_inc(p32_made, 1)
            dve.wait_ge(phi_made, 1)
            nc.vector.tensor_tensor(p_lo[:], p32[:], p_hi[:].bitcast(F32), ALU.subtract).then_inc(plo_made, 1)

            low(4)
            low(5)
            b_split(1, 3)
            low(6)
            low(7)
            b_split(2, 2)
            low(8)
            low(9)
            b_split(3, 1)
            xl = b32[:, 4]
            for h in range(NH):
                dve.wait_ge(lin_done, h + 1)
                dve.wait_ge(x1b_made, h + 1)
                nc.vector.tensor_tensor(xl[:, h], lin_ps[h][:], x1[:, h], ALU.add).then_inc(xl_made, 1)
            for h in range(NH):
                dve.wait_ge(y_done, NH * 4 + h + 1)
                dve.wait_ge(b2c_made, h + 1)
                nc.vector.tensor_tensor(act_out[:, h], z_ps[0][h][:], b32[:, 0, h],
                                        ALU.subtract).then_inc(g_made, 1)
                dve.wait_ge(g_made, h + 1)
                nc.vector.scalar_tensor_tensor(out=leaky[:, h], in0=act_out[:, h], scalar=0.01,
                                               in1=act_out[:, h], op0=ALU.mult, op1=ALU.max).then_inc(leaky_made, 1)
                dve.wait_ge(leaky_made, h + 1)
                dve.wait_ge(xl_made, h + 1)
                nc.vector.tensor_tensor(res[:, h], leaky[:, h], xl[:, h], ALU.add).then_inc(res_made, 1)

        @block.tensor
        def _(pe):
            def count_chunk(c, first, last):
                for q in range(NH):
                    mm = nc.tensor.matmul(count_ps[q][:, 0:N], onehot[:, c, 1, q * P:(q + 1) * P],
                                          onehot[:, c, 0], start=first, stop=last)
                return mm

            def count_group(g, first=False, last=False):
                for j in range(GRP):
                    pe.wait_ge(onehots, g * GRP + j + 1)
                    mm = count_chunk(g * GRP + j, first and j == 0, last and j == GRP - 1)
                return mm

            count_group(0, first=True)
            pe.wait_ge(eye_made, 1)
            for h in range(NH):
                pe.wait_ge(u_made, h + 1)
                for c in range(DC):
                    mm = nc.tensor.transpose(t_ps[c // 2][:, (c % 2) * N + h * P:(c % 2) * N + (h + 1) * P],
                                             u[:, h, c * P:(c + 1) * P], eye[:, P:2 * P])
                mm.then_inc(turned, 1)
            with pe.Fori(1, NG - 1) as g:
                count_group(g)

            def low_wait(s):
                if low_count(s, "pool"):
                    pe.wait_ge(wlo_pool, low_count(s, "pool"))
                if low_count(s, "dve"):
                    pe.wait_ge(wlo_dve, low_count(s, "dve"))

            def times_weight(ps, s, h, terms, first, last):
                slot = W_SLOT[s]
                for n, (a, w) in enumerate(terms):
                    for c in range(DC):
                        mm = nc.tensor.matmul(ps[h][:], (t_hi, t_lo)[a][:, c, h * P:(h + 1) * P],
                                              (w_hi, w_lo)[w][slot][:, c],
                                              start=first and n == 0 and c == 0,
                                              stop=last and n == len(terms) - 1 and c == DC - 1)
                return mm

            pe.wait_ge(thi_made, 2)
            pe.wait_ge(whi_made, PIECE)
            for h in range(NH):
                times_weight(sup_ps, 0, h, [(0, 0)], True, False)
            low_wait(0)
            for h in range(NH):
                times_weight(sup_ps, 0, h, [(0, 1)], False, False)
            count_group(NG - 1, last=True).then_inc(counted, 1)
            pe.wait_ge(tlo_made, 2)
            for h in range(NH):
                times_weight(sup_ps, 0, h, [(1, 0)], False, True).then_inc(sup_done, 1)
            pe.wait_ge(adj_made, NH)
            pe.wait_ge(onesr_made, 1)
            for h in range(NH):
                for q in range(NH):
                    mm = nc.tensor.matmul(deg_ps[:, 2 * h:2 * h + 2], adj[:, q, h * P:(h + 1) * P], ones_r[:],
                                          start=q == 0, stop=q == NH - 1)
            mm.then_inc(deg_done, 1)

            def weighted(g):
                pe.wait_ge(srcs, g + 1)
                if g in LOW_BY_ACT:
                    pe.wait_ge(wdst_lo_act, LOW_BY_ACT.index(g) + 1)
                else:
                    pe.wait_ge(wdst_lo, g + 1 - sum(a < g for a in LOW_BY_ACT))
                for j in range(GRP):
                    c = g * GRP + j
                    pe.wait_ge(wdst_hi, c + 1)
                    for m in range(NH):
                        mm = nc.tensor.matmul(aw_ps[m][:], src_r[:, g % 2, j, m * P:(m + 1) * P],
                                              wdst_r[:, c].rearrange("p t n -> p (t n)"),
                                              start=c == 0, stop=c == EC - 1)
                        if c == EC - 1:
                            mm.then_inc(aw_done, 1)
                if c < EC - 1:
                    mm.then_inc(srcs_used, 1)

            weighted(0)

            pe.wait_ge(deg_copied, 1)
            for h in range(NH):
                for part, made, tile in ((0, suphi_made, sup_hi), (1, suplo_made, sup_lo)):
                    for q in range(NH):
                        pe.wait_ge(made, q + 1)
                        mm = nc.tensor.matmul(agg_ps[h][:], adj[:, q, h * P:(h + 1) * P], tile[:, q],
                                              start=part == 0 and q == 0, stop=part == 1 and q == NH - 1)
                mm.then_inc(agg_done, 1)

            weighted(1)
            weighted(2)

            for h in range(NH):
                pe.wait_ge(xn_made, h + 1)
                pe.wait_ge(tlo_made, 2)
                for c in range(DC):
                    mm = nc.tensor.transpose(t_ps[c // 2][:, (c % 2) * N + h * P:(c % 2) * N + (h + 1) * P],
                                             u[:, h, c * P:(c + 1) * P], eye[:, P:2 * P])
                mm.then_inc(xturned, 1)

            def z_term(s, ps, closes):
                pe.wait_ge(whi_made, PIECE * (s + 1))
                for h in range(NH):
                    times_weight(ps, s, h, [(0, 0), (1, 0)], True, False)
                low_wait(s)
                for h in range(NH):
                    mm = times_weight(ps, s, h, [(0, 1)], False, closes is not None)
                    if closes is not None:
                        mm.then_inc(closes, 1)
                    elif h == NH - 1:
                        mm.then_inc(z_done, 1)

            def propagate(i, k):
                hi, lo = b_hi[(i - 1) % 2], b_lo[(i - 1) % 2]
                for h in range(NH):
                    for n, (pt, bt, made) in enumerate(((p_hi, hi, bhi_made), (p_lo, hi, bhi_made),
                                                        (p_hi, lo, blo_made))):
                        for m in range(NH):
                            pe.wait_ge(made, NH * (i - 1) + m + 1)
                            mm = nc.tensor.matmul(z_ps[k][h][:], pt[:, m, h * P:(h + 1) * P], bt[:, m],
                                                  start=False, stop=n == 2 and m == NH - 1)
                    mm.then_inc(y_done, 1)

            pe.wait_ge(xlo_made, 2)
            pe.wait_ge(x1_made, NH)
            z_term(1, z_ps[4], y_done)
            weighted(3)
            z_term(2, z_ps[3], None)
            pe.wait_ge(ones_made, 1)
            pe.wait_ge(diag_made, NH)
            nc.tensor.matmul(bc_ps[:, 0:N], ones[:], diag[:].rearrange("p h n -> p (h n)"), start=True,
                             stop=True).then_inc(bc_done, 1)
            z_term(3, z_ps[2], None)
            pe.wait_ge(plo_made, 1)
            propagate(1, 3)
            z_term(4, z_ps[1], None)
            propagate(2, 2)
            z_term(5, z_ps[0], None)
            propagate(3, 1)
            z_term(6, lin_ps, lin_done)
            propagate(4, 0)


def kernel(x, src, dst, edge_weight, L0_gnn_weight, L0_gnn_bias, L1_gnn_ln_gamma, L1_gnn_ln_beta,
           L1_gnn_cheb_W, L1_gnn_cheb_b, L1_gnn_lin_W, L1_gnn_lin_b):
    import concourse.bacc as bacc
    from concourse.bass_utils import run_bass_kernel_spmd

    a = {k: np.asarray(v) for k, v in locals().items() if k not in ("bacc", "run_bass_kernel_spmd")}
    cheb = a["L1_gnn_cheb_W"]
    arrays = {
        "x": a["x"],
        "edges": np.stack([a["src"].reshape(P, EC), a["dst"].reshape(P, EC)], axis=1),
        "edge_w": a["edge_weight"].reshape(P, EC),
        "w0": a["L0_gnn_weight"],
        "wt": np.stack([cheb[k].T for k in range(K - 1, -1, -1)] + [a["L1_gnn_lin_W"].T]),
        "cols": np.stack([a[n].reshape(DC, P).T for n in ("L1_gnn_ln_gamma", "L1_gnn_ln_beta")], axis=1),
        "rows": np.broadcast_to(np.stack([a["L0_gnn_bias"], a["L1_gnn_cheb_b"], a["L1_gnn_lin_b"]]), (P, 3, D)),
    }
    arrays = {n: np.ascontiguousarray(v) for n, v in arrays.items()}
    nc = bacc.Bacc("TRN2", target_bir_lowering=False, num_devices=1)
    aps = [nc.dram_tensor(n, v.shape, mybir.dt.from_np(v.dtype), kind="ExternalInput").ap()
           for n, v in arrays.items()]
    aps.append(nc.dram_tensor("out", (N, D), F32, kind="ExternalOutput").ap())
    build(nc, *aps)
    return run_bass_kernel_spmd(nc, [arrays], core_ids=[0]).results[0]["out"]
```

```python
from contextlib import ExitStack

import numpy as np

import concourse.bass as bass
import concourse.mybir as mybir

F32 = mybir.dt.float32
F32R = mybir.dt.float32r
BF16 = mybir.dt.bfloat16
I32 = mybir.dt.int32
ALU = mybir.AluOpType
ACT = mybir.ActivationFunctionType

P = 128
N = 256
NH = N // P
E = 4096
EC = E // P
D = 512
DC = D // P
K = 5
EPS = 1e-5
GRP = 8
NG = EC // GRP
LOW_BY_ACT = range(6, 8)

NW = 1 + K + 1
LIN = NW - 1
W_SLOT = [0, 1, 0, 1, 2, 3, 0]
RAW = 2
PIECE = 2
PC = DC // PIECE
B_SCALE = {k: 0.5 if k == 1 else 1.0 for k in range(1, K)}
WARM_MATMULS = 12
OUT_PARTS = [(0, slice(0, D)), (1, slice(0, D // 2)), (1, slice(D // 2, D))]


def build(nc, x, edges, edge_w, w0, wt, cols, rows, out):
    ctx = ExitStack()
    with ctx:
        def sb(name, shape, dt, where=ctx):
            return where.enter_context(nc.sbuf_tensor(name, shape, dt))

        def sem(name):
            return ctx.enter_context(nc.semaphore(name))

        x_sb = sb("x_sb", [P, NH, D], F32)
        x1 = sb("x1", [P, NH, D], F32)
        u = sb("u", [P, NH, D], F32)
        row_bias = sb("row_bias", [P, 3, D], F32)
        col_gb = sb("col_gb", [P, 2, DC], F32)
        t32 = sb("t32", [P, DC, N], F32)
        t_hi = sb("t_hi", [P, DC, N], F32R)
        t_lo = sb("t_lo", [P, DC, N], F32R)
        raw = sb("raw", [P, RAW, DC, D], F32)
        w_hi = [sb(f"w_hi{i}", [P, DC, D], F32R) for i in range(2)]
        w_lo = [sb(f"w_lo{i}", [P, DC, D], F32R) for i in range(2)]
        sup_hi = sb("sup_hi", [P, NH, D], F32R)
        sup_lo = sb("sup_lo", [P, NH, D], F32R)
        adj = sb("adj", [P, NH, N], F32R)
        iota_i = sb("iota_i", [P, N], I32)
        iota = sb("iota", [P, N], BF16)
        warm = sb("warm", [P, N], BF16)
        eye = sb("eye", [P, P + N], F32)
        ones = sb("ones", [P, P], F32)
        ones_r = sb("ones_r", [P, 2], F32R)
        half_neg = sb("half_neg", [P, NH], F32)
        ed_i = sb("ed_i", [P, EC, 2], I32)
        ed = sb("ed", [P, EC, 2, 2], BF16)
        ew = sb("ew", [P, EC], F32)
        ew_hi = sb("ew_hi", [P, EC], F32R)
        ew_lo = sb("ew_lo", [P, EC], F32)
        x_sum = sb("x_sum", [P, NH], F32)
        x_nmean = sb("x_nmean", [P, NH], F32)
        x_sq = sb("x_sq", [P, NH], F32)
        x1_sum = sb("x1_sum", [P, NH], F32)
        x1_nmean = sb("x1_nmean", [P, NH], F32)
        x1_sq = sb("x1_sq", [P, NH], F32)
        scratch = sb("scratch", [P, D], F32)
        stats = sb("stats", [P, NH, 6], F32)
        mv = sb("mv", [P, NH, 2], F32)
        ve = sb("ve", [P, 2, NH], F32)
        rs = sb("rs", [P, 2, NH], F32)
        eps1 = sb("eps1", [P, NH], F32)
        deg0 = sb("deg0", [P, NH], F32)
        dn = sb("dn", [P, NH], F32)
        sup_scale = sb("sup_scale", [P, NH], F32)
        degw = sb("degw", [P, NH], F32)
        deg_not = sb("deg_not", [P, NH], F32)
        deg_safe = sb("deg_safe", [P, NH], F32)
        dpow = sb("dpow", [P, NH], F32)
        dinv = sb("dinv", [P, NH], F32)
        dinv_m2 = sb("dinv_m2", [P, NH], F32)

        edge_mem = ExitStack()
        onehot = sb("onehot", [P, EC, 2, N], BF16, edge_mem)
        wdst_r = sb("wdst_r", [P, EC, 2, N], F32R, edge_mem)
        src_r = sb("src_r", [P, 2, GRP, N], F32R, edge_mem)
        edge_mem.close()
        w_hi += [sb(f"w_hi{i}", [P, DC, D], F32R) for i in (2, 3)]
        w_lo += [sb(f"w_lo{i}", [P, DC, D], F32R) for i in (2, 3)]
        a_lo = sb("a_lo", [P, NH, N], F32)
        aw = sb("aw", [P, NH, N], F32)
        diag = sb("diag", [P, NH, P], F32)
        p32 = sb("p32", [P, NH, N], F32)
        p_hi = sb("p_hi", [P, NH, N], F32R)
        p_lo = sb("p_lo", [P, NH, N], F32R)
        b_mem = sb("b_mem", [P, K - 1, NH, D], F32)
        b32 = [b_mem[:, k] for k in range(K - 1)] + [x_sb]
        b_hi = [sup_hi, sb("b_hi1", [P, NH, D], F32R)]
        b_lo = [sup_lo, sb("b_lo1", [P, NH, D], F32R)]
        xl = sb("xl", [P, NH, D], F32)
        act_out = sb("act_out", [P, NH, D], F32)
        leaky = sb("leaky", [P, NH, D], F32)
        res = sb("res", [P, NH, D], F32)

        bank = [ctx.enter_context(nc.psum_tensor(f"bank{i}", [P, D], F32)) for i in range(8)]
        pair_a, pair_b, pair_c, pair_d = (bank[2 * i:2 * i + 2] for i in range(4))
        count_ps, agg_ps = pair_a, pair_a
        t_ps = pair_b
        sup_ps, aw_ps = pair_c, pair_d
        deg_ps, bc_ps = pair_a[0], pair_a[0]
        z_ps = {4: pair_a, 3: pair_b, 2: pair_c, 1: pair_d, 0: pair_a}
        lin_ps = pair_b

        in_edges, in_ew, in_cols = sem("in_edges"), sem("in_ew"), sem("in_cols")
        in_bias0, in_bias1 = sem("in_bias0"), sem("in_bias1")
        in_x = [sem(f"in_x{i}") for i in range(NH)]
        in_w = [sem(f"in_w{i}") for i in range(RAW)]
        out_done = sem("out_done")
        iota_made, iota_cast, eye_clear, eye_made, ones_made, onesr_made, half_made = (sem(n) for n in (
            "iota_made", "iota_cast", "eye_clear", "eye_made", "ones_made", "onesr_made", "half_made"))
        edges_cast, ew_hi_made, ew_ready = sem("edges_cast"), sem("ew_hi_made"), sem("ew_ready")
        warm_made = sem("warm_made")
        onehots = sem("onehots")
        wdst_hi, wdst_lo, wdst_lo_act = sem("wdst_hi"), sem("wdst_lo"), sem("wdst_lo_act")
        srcs = sem("srcs")
        srcs_used = sem("srcs_used")
        stats_made, mv_made, u_made, ve_made, rs_made, eps1_made = (sem(n) for n in (
            "stats_made", "mv_made", "u_made", "ve_made", "rs_made", "eps1_made"))
        xb_made = sem("xb_made")
        sum_made, mean_made, sq_made = sem("sum_made"), sem("mean_made"), sem("sq_made")
        mean1_made, sq1_made = sem("mean1_made"), sem("sq1_made")
        u1_made_act, u1_made_dve = sem("u1_made_act"), sem("u1_made_dve")
        whi_made, wlo_made = sem("whi_made"), sem("wlo_made")
        turned, thi_made, tlo_made = sem("turned"), sem("thi_made"), sem("tlo_made")
        counted, adj_made, deg_done, deg_copied, dn_made, sscale_made = (sem(n) for n in (
            "counted", "adj_made", "deg_done", "deg_copied", "dn_made", "sscale_made"))
        sup_done, suphi_made, suplo_made, agg_done, x1_made, x1b_made = (sem(n) for n in (
            "sup_done", "suphi_made", "suplo_made", "agg_done", "x1_made", "x1b_made"))
        xn_made, xturned, t32_made, t32_made_dve, xhi_made, xhi_made_act, xlo_made = (sem(n) for n in (
            "xn_made", "xturned", "t32_made", "t32_made_dve", "xhi_made", "xhi_made_act", "xlo_made"))
        aw_done, alo_made, aw_made, guard1, guard2, dpow_made, dinv_made, dinv2_made = (sem(n) for n in (
            "aw_done", "alo_made", "aw_made", "guard1", "guard2", "dpow_made", "dinv_made", "dinv2_made"))
        diag_made, bc_done, p32_made, phi_made, plo_made = (sem(n) for n in (
            "diag_made", "bc_done", "p32_made", "phi_made", "plo_made"))
        z_done = sem("z_done")
        y_done = sem("y_done")
        b32_made, bhi_made, blo_made = sem("b32_made"), sem("bhi_made"), sem("blo_made")
        b2c_made, lin_done, xl_made, g_made, leaky_made, res_made = (sem(n) for n in (
            "b2c_made", "lin_done", "xl_made", "g_made", "leaky_made", "res_made"))

        block = ctx.enter_context(nc.Block())

        @block.sync
        def _(sp):
            sp.dma_start(ed_i[:], edges).then_inc(in_edges, 16)
            for h in range(NH):
                sp.dma_start(x_sb[:, h], x[h * P:(h + 1) * P, :]).then_inc(in_x[h], 16)
            sp.dma_start(ew[:], edge_w).then_inc(in_ew, 16)
            for s in range(NW):
                src = w0 if s == 0 else wt[s - 1]
                if s >= RAW:
                    sp.wait_ge(whi_made, PIECE * (s - RAW + 1))
                    sp.wait_ge(wlo_made, PIECE * (s - RAW + 1))
                sp.dma_start(raw[:, s % RAW], src.rearrange("(c p) f -> p c f", p=P)).then_inc(in_w[s % RAW], 16)
                if s == 0:
                    sp.dma_start(row_bias[:, 0:1], rows[:, 0:1]).then_inc(in_bias0, 16)
                    sp.dma_start(col_gb[:], cols).then_inc(in_cols, 16)
                elif s == RAW:
                    sp.dma_start(row_bias[:, 1:3], rows[:, 1:3]).then_inc(in_bias1, 16)
            for n, (h, span) in enumerate(OUT_PARTS):
                sp.wait_ge(res_made, n + 1)
                sp.dma_start(out[h * P:(h + 1) * P, span], res[:, h, span]).then_inc(out_done, 16)
            sp.wait_ge(out_done, 16 * len(OUT_PARTS))

        @block.gpsimd
        def _(pool):
            nc.gpsimd.iota(iota_i[:], pattern=[[1, N]], base=0, channel_multiplier=0).then_inc(iota_made, 1)
            nc.gpsimd.memset(eye[:], 0.0).then_inc(eye_clear, 1)
            nc.gpsimd.memset(half_neg[:], -0.5).then_inc(half_made, 1)
            pool.wait_ge(eye_clear, 1)
            nc.gpsimd.affine_select(out=eye[:], in_=eye[:], compare_op=ALU.not_equal, fill=1.0, base=P,
                                    pattern=[[-1, P + N]], channel_multiplier=1).then_inc(eye_made, 1)
            nc.gpsimd.memset(ones[:], 1.0).then_inc(ones_made, 1)

            pool.wait_ge(half_made, 1)
            pool.wait_ge(ve_made, 1)
            nc.gpsimd.tensor_tensor(rs[:, 0], ve[:, 0], half_neg[:], ALU.pow).then_inc(rs_made, 1)
            pool.wait_ge(deg_copied, 1)
            nc.gpsimd.tensor_tensor(dn[:], deg0[:], half_neg[:], ALU.pow).then_inc(dn_made, 1)
            pool.wait_ge(rs_made, 1)
            pool.wait_ge(dn_made, 1)
            nc.gpsimd.tensor_tensor(sup_scale[:], dn[:], rs[:, 0], ALU.mult).then_inc(sscale_made, 1)
            pool.wait_ge(ve_made, 2)
            nc.gpsimd.tensor_tensor(rs[:, 1], ve[:, 1], half_neg[:], ALU.pow).then_inc(rs_made, 1)
            pool.wait_ge(guard2, 1)
            nc.gpsimd.tensor_tensor(dpow[:], deg_safe[:], half_neg[:], ALU.pow).then_inc(dpow_made, 1)

        @block.scalar
        def _(act):
            def high(s):
                slot = W_SLOT[s]
                act.wait_ge(in_w[s % RAW], 16 * (s // RAW + 1))
                if s == 2:
                    act.wait_ge(sup_done, NH)
                elif slot >= 2:
                    act.wait_ge(aw_done, NH)
                elif s == 3:
                    act.wait_ge(y_done, NH)
                elif s == 6:
                    act.wait_ge(z_done, 1)
                for p in range(PIECE):
                    part = slice(p * PC, (p + 1) * PC)
                    nc.scalar.activation(w_hi[slot][:, part], raw[:, s % RAW, part], ACT.Copy).then_inc(whi_made, 1)

            def wdst(part, chunks):
                scale, made = ((ew_hi[:].bitcast(F32), wdst_hi), (ew_lo[:], wdst_lo_act))[part]
                act.wait_ge(ew_ready, 1)
                for c in chunks:
                    act.wait_ge(onehots, c + 1)
                    nc.scalar.activation(wdst_r[:, c, part], onehot[:, c, 1], ACT.Copy,
                                         scale=scale[:, c:c + 1]).then_inc(made, 1)

            def src_chunks(first, count):
                g, at = first // GRP, first % GRP
                act.wait_ge(onehots, first + count)
                if g >= 2:
                    act.wait_ge(srcs_used, g - 1)
                nc.scalar.activation(src_r[:, g % 2, at:at + count], onehot[:, first:first + count, 0],
                                     ACT.Copy).then_inc(srcs, count)

            for h in range(NH):
                act.wait_ge(in_x[h], 16)
                nc.scalar.activation(scratch[:], x_sb[:, h], ACT.Copy, accum_out=x_sum[:, h:h + 1]).then_inc(sum_made, 1)
                act.wait_ge(sum_made, h + 1)
            for h in range(NH):
                act.wait_ge(mean_made, h + 1)
                nc.scalar.activation(u[:, h], x_sb[:, h], ACT.Relu, bias=x_nmean[:, h:h + 1]).then_inc(u_made, 1)
            for h in range(NH):
                nc.scalar.activation(scratch[:], x_sb[:, h], ACT.Square, bias=x_nmean[:, h:h + 1],
                                     accum_out=x_sq[:, h:h + 1]).then_inc(sq_made, 1)
                act.wait_ge(sq_made, h + 1)
            high(0)
            for i in range(2):
                act.wait_ge(turned, NH)
                nc.scalar.activation(t_hi[:, 2 * i:2 * i + 2], t_ps[i][:].rearrange("p (c n) -> p c n", c=2),
                                     ACT.Copy).then_inc(thi_made, 1)
            wdst(0, range(13))
            act.wait_ge(deg_done, 1)
            nc.scalar.activation(deg0[:], deg_ps[:, 0:2 * NH].rearrange("p (h t) -> p h t", t=2)[:, :, 0],
                                 ACT.Copy).then_inc(deg_copied, 1)
            src_chunks(0, 4)
            wdst(0, range(13, 14))
            for h in range(NH):
                act.wait_ge(sscale_made, 1)
                act.wait_ge(sup_done, h + 1)
                nc.scalar.activation(sup_hi[:, h], sup_ps[h][:], ACT.Copy,
                                     scale=sup_scale[:, h:h + 1]).then_inc(suphi_made, 1)
            src_chunks(4, 4)
            wdst(1, LOW_BY_ACT)
            wdst(0, range(14, 16))
            act.wait_ge(mean1_made, 1)
            nc.scalar.activation(u[:, 0], x1[:, 0], ACT.Relu, bias=x1_nmean[:, 0:1]).then_inc(u1_made_act, 1)
            for h in range(NH):
                act.wait_ge(mean1_made, h + 1)
                if h:
                    act.wait_ge(sq1_made, h)
                nc.scalar.activation(scratch[:], x1[:, h], ACT.Square, bias=x1_nmean[:, h:h + 1],
                                     accum_out=x1_sq[:, h:h + 1]).then_inc(sq1_made, 1)
            high(1)
            src_chunks(8, 4)
            wdst(0, range(16, 17))
            act.wait_ge(in_cols, 16)
            act.wait_ge(xturned, NH)
            act.wait_ge(sup_done, NH)
            for dest, made in ((t_hi, xhi_made_act), (t32, t32_made)):
                for c in range(DC // 2):
                    nc.scalar.activation(dest[:, c], t_ps[c // 2][:, (c % 2) * N:(c % 2 + 1) * N], ACT.Identity,
                                         scale=col_gb[:, 0, c:c + 1], bias=col_gb[:, 1, c:c + 1]).then_inc(made, 1)

            def b_copy(i, k):
                for h in range(NH):
                    act.wait_ge(y_done, NH * i + h + 1)
                    nc.scalar.activation(b32[k][:, h], z_ps[k][h][:], ACT.Copy).then_inc(b32_made, 1)

            src_chunks(12, 4)
            high(2)
            wdst(0, range(17, 24))
            src_chunks(16, 8)
            b_copy(0, 4)
            wdst(0, range(24, 32))
            src_chunks(24, 8)
            high(3)
            for h in range(NH):
                act.wait_ge(aw_done, h + 1)
                nc.scalar.activation(a_lo[:, h], aw_ps[h][:, N:2 * N], ACT.Copy).then_inc(alo_made, 1)
            high(4)
            act.wait_ge(p32_made, NH)
            nc.scalar.activation(p_hi[:], p32[:], ACT.Copy).then_inc(phi_made, 1)
            high(5)
            b_copy(1, 3)
            high(6)
            for i, k in ((2, 2), (3, 1)):
                for h in range(NH):
                    act.wait_ge(b32_made, NH * i + h + 1)
                    act.wait_ge(y_done, NH * i)
                    nc.scalar.activation(b_hi[i % 2][:, h], b32[k][:, h], ACT.Copy,
                                         scale=B_SCALE[k]).then_inc(bhi_made, 1)

        @block.vector
        def _(dve):
            nc.vector.memset(warm[:], 0.0).then_inc(warm_made, 1)
            nc.vector.memset(ones_r[:].bitcast(F32), 1.0).then_inc(onesr_made, 1)
            dve.wait_ge(iota_made, 1)
            nc.vector.tensor_copy(iota[:], iota_i[:]).then_inc(iota_cast, 1)
            dve.wait_ge(in_edges, 16)
            nc.vector.tensor_copy(ed[:], ed_i[:].unsqueeze(3).broadcast_to([P, EC, 2, 2])).then_inc(edges_cast, 1)
            dve.wait_ge(edges_cast, 1)
            dve.wait_ge(iota_cast, 1)

            def onehot_chunks(first, count):
                rows = 2 * count
                pairs = [P, rows, N // 2, 2]
                nodes = iota[:].rearrange("p (m t) -> p m t", t=2).unsqueeze(1).broadcast_to(pairs)
                ends = ed[:, first:first + count].rearrange("p c s t -> p (c s) t").unsqueeze(2).broadcast_to(pairs)
                rows_out = onehot[:, first:first + count].rearrange("p c s (m t) -> p (c s) m t", t=2)
                nc.vector.tensor_tensor(rows_out, nodes, ends, ALU.is_equal).then_inc(onehots, count)

            def wdst_low(first, count):
                chunks = slice(first, first + count)
                dve.wait_ge(ew_ready, 1)
                dve.wait_ge(onehots, first + count)
                nc.vector.tensor_tensor(wdst_r[:, chunks, 1], onehot[:, chunks, 1],
                                        ew_lo[:, chunks].unsqueeze(2).broadcast_to([P, count, N]),
                                        ALU.mult).then_inc(wdst_lo, count)

            def low(s, p):
                part = slice(p * PC, (p + 1) * PC)
                slot = W_SLOT[s]
                dve.wait_ge(whi_made, PIECE * s + p + 1)
                nc.vector.tensor_tensor(w_lo[slot][:, part], raw[:, s % RAW, part],
                                        w_hi[slot][:, part].bitcast(F32), ALU.subtract).then_inc(wlo_made, 1)

            for first, count in ((0, 1), (1, 1), (2, 2), (4, 2), (6, 2)):
                onehot_chunks(first, count)
            for h in range(NH):
                dve.wait_ge(sum_made, h + 1)
                nc.vector.tensor_scalar(x_nmean[:, h:h + 1], x_sum[:, h:h + 1], -1.0 / D, None,
                                        ALU.mult).then_inc(mean_made, 1)
            dve.wait_ge(in_ew, 16)
            nc.vector.tensor_copy(ew_hi[:], ew[:]).then_inc(ew_hi_made, 1)
            onehot_chunks(GRP, 4)
            dve.wait_ge(ew_hi_made, 1)
            nc.vector.tensor_tensor(ew_lo[:], ew[:], ew_hi[:].bitcast(F32), ALU.subtract).then_inc(ew_ready, 1)
            for c in range(GRP + 4, EC, 4):
                onehot_chunks(c, 4)
            dve.wait_ge(sq_made, NH)
            nc.vector.tensor_scalar(ve[:, 0], x_sq[:], 1.0 / D, EPS, ALU.mult, ALU.add).then_inc(ve_made, 1)
            low(0, 0)
            for i in range(2):
                dve.wait_ge(thi_made, i + 1)
                nc.vector.tensor_tensor(t_lo[:, 2 * i:2 * i + 2], t_ps[i][:].rearrange("p (c n) -> p c n", c=2),
                                        t_hi[:, 2 * i:2 * i + 2].bitcast(F32), ALU.subtract).then_inc(tlo_made, 1)
            dve.wait_ge(eye_made, 1)
            for q in range(NH):
                dve.wait_ge(counted, 1)
                nc.vector.scalar_tensor_tensor(out=adj[:, q], in0=count_ps[q][:, 0:N], scalar=1.0,
                                               in1=eye[:, P - q * P:P - q * P + N], op0=ALU.min,
                                               op1=ALU.add).then_inc(adj_made, 1)
            low(0, 1)
            dve.wait_ge(in_bias0, 16)
            for h in range(NH):
                nc.vector.tensor_tensor(x_sb[:, h], x_sb[:, h], row_bias[:, 0], ALU.add).then_inc(xb_made, 1)
            wdst_low(0, 4)
            for h in range(NH):
                dve.wait_ge(suphi_made, h + 1)
                nc.vector.scalar_tensor_tensor(out=sup_lo[:, h], in0=sup_ps[h][:], scalar=sup_scale[:, h:h + 1],
                                               in1=sup_hi[:, h].bitcast(F32), op0=ALU.mult,
                                               op1=ALU.subtract).then_inc(suplo_made, 1)
            wdst_low(4, 2)
            dve.wait_ge(dn_made, 1)
            for h in range(NH):
                dve.wait_ge(agg_done, h + 1)
                dve.wait_ge(xb_made, h + 1)
                nc.vector.scalar_tensor_tensor(out=x1[:, h], in0=agg_ps[h][:], scalar=dn[:, h:h + 1],
                                               in1=x_sb[:, h], op0=ALU.mult, op1=ALU.add,
                                               accum_out=x1_sum[:, h:h + 1]).then_inc(x1_made, 1)
                dve.wait_ge(x1_made, h + 1)
                nc.vector.tensor_scalar(x1_nmean[:, h:h + 1], x1_sum[:, h:h + 1], -1.0 / D, None,
                                        ALU.mult).then_inc(mean1_made, 1)
            dve.wait_ge(mean1_made, 2)
            nc.vector.tensor_scalar(u[:, 1], x1[:, 1], x1_nmean[:, 1:2], 0.0,
                                    ALU.add, ALU.max).then_inc(u1_made_dve, 1)
            for h, made in enumerate((u1_made_act, u1_made_dve)):
                dve.wait_ge(made, 1)
                nc.vector.bn_stats(stats[:, h], u[:, h]).then_inc(stats_made, 1)
            dve.wait_ge(sq1_made, NH)
            nc.vector.tensor_scalar(eps1[:], x1_sq[:], EPS / D, EPS * EPS, ALU.mult, ALU.add).then_inc(eps1_made, 1)
            for h in range(NH):
                dve.wait_ge(stats_made, h + 1)
                nc.vector.bn_aggr(mv[:, h], stats[:, h]).then_inc(mv_made, 1)
            dve.wait_ge(mv_made, NH)
            dve.wait_ge(eps1_made, 1)
            nc.vector.tensor_tensor(ve[:, 1], mv[:, :, 1], eps1[:], ALU.add).then_inc(ve_made, 1)
            wdst_low(8, 2)
            for h in range(NH):
                dve.wait_ge(rs_made, 2)
                nc.vector.tensor_scalar(u[:, h], u[:, h], mv[:, h, 0:1], rs[:, 1, h:h + 1],
                                        ALU.subtract, ALU.mult).then_inc(xn_made, 1)
            wdst_low(10, 2)
            dve.wait_ge(in_cols, 16)
            dve.wait_ge(xturned, NH)
            for c in range(DC // 2, DC):
                nc.vector.tensor_scalar(t32[:, c], t_ps[c // 2][:, (c % 2) * N:(c % 2 + 1) * N],
                                        col_gb[:, 0, c:c + 1], col_gb[:, 1, c:c + 1],
                                        ALU.mult, ALU.add).then_inc(t32_made_dve, 1)
            dve.wait_ge(t32_made_dve, DC // 2)
            dve.wait_ge(sup_done, NH)
            nc.vector.tensor_copy(t_hi[:, 2:4], t32[:, 2:4]).then_inc(xhi_made, 1)
            for part in (slice(2, 4), slice(0, 2)):
                if part.start:
                    dve.wait_ge(xhi_made, 1)
                else:
                    dve.wait_ge(xhi_made_act, DC // 2)
                    dve.wait_ge(t32_made, DC // 2)
                nc.vector.tensor_tensor(t_lo[:, part], t32[:, part], t_hi[:, part].bitcast(F32),
                                        ALU.subtract).then_inc(xlo_made, 1)

            def b2_less_bias(h):
                nc.vector.tensor_tensor(b32[0][:, h], b32[2][:, h], row_bias[:, 1],
                                        ALU.subtract).then_inc(b2c_made, 1)

            def b_step(i, k, between=None):
                for h in range(NH):
                    if between and h == 1:
                        between()
                    dve.wait_ge(y_done, NH * i + h + 1)
                    nc.vector.tensor_tensor(b32[k][:, h], z_ps[k][h][:], b32[k + 2][:, h],
                                            ALU.subtract).then_inc(b32_made, 1)

            def b_high(i, k, h):
                dve.wait_ge(b32_made, NH * i + h + 1)
                nc.vector.tensor_copy(b_hi[i % 2][:, h], b32[k][:, h]).then_inc(bhi_made, 1)

            def b_low(i, k, h):
                hi = b_hi[i % 2][:, h].bitcast(F32)
                dve.wait_ge(b32_made, NH * i + h + 1)
                dve.wait_ge(bhi_made, NH * i + h + 1)
                nc.vector.scalar_tensor_tensor(out=b_lo[i % 2][:, h], in0=b32[k][:, h], scalar=B_SCALE[k],
                                               in1=hi, op0=ALU.mult, op1=ALU.subtract).then_inc(blo_made, 1)

            wdst_low(12, 4)
            low(1, 0)
            low(1, 1)
            wdst_low(16, 4)
            low(2, 0)
            low(2, 1)
            wdst_low(20, 4)
            wdst_low(24, 4)
            wdst_low(28, 4)
            for h in range(NH):
                b_high(0, 4, h)
                b_low(0, 4, h)
            low(3, 0)
            low(3, 1)
            dve.wait_ge(in_bias1, 16)
            for h in range(NH):
                nc.vector.tensor_tensor(x1[:, h], x1[:, h], row_bias[:, 2], ALU.add).then_inc(x1b_made, 1)
            for h in range(NH):
                dve.wait_ge(alo_made, h + 1)
                nc.vector.scalar_tensor_tensor(out=aw[:, h], in0=aw_ps[h][:, 0:N], scalar=1.0, in1=a_lo[:, h],
                                               op0=ALU.mult, op1=ALU.add,
                                               accum_out=degw[:, h:h + 1]).then_inc(aw_made, 1)
            dve.wait_ge(aw_made, NH)
            nc.vector.tensor_scalar(deg_not[:], degw[:], 0.0, None, ALU.is_le).then_inc(guard1, 1)
            dve.wait_ge(guard1, 1)
            nc.vector.scalar_tensor_tensor(out=deg_safe[:], in0=degw[:], scalar=0.0, in1=deg_not[:],
                                           op0=ALU.max, op1=ALU.add).then_inc(guard2, 1)
            dve.wait_ge(dpow_made, 1)
            nc.vector.scalar_tensor_tensor(out=dinv[:], in0=degw[:], scalar=0.0, in1=dpow[:],
                                           op0=ALU.is_gt, op1=ALU.mult).then_inc(dinv_made, 1)
            dve.wait_ge(dinv_made, 1)
            nc.vector.tensor_scalar(dinv_m2[:], dinv[:], -2.0, None, ALU.mult).then_inc(dinv2_made, 1)
            for h in range(NH):
                nc.vector.tensor_scalar(diag[:, h], eye[:, P:2 * P], dinv[:, h:h + 1], None,
                                        ALU.mult).then_inc(diag_made, 1)
            dve.wait_ge(dinv2_made, 1)
            dve.wait_ge(bc_done, 1)
            for h in range(NH):
                nc.vector.scalar_tensor_tensor(out=p32[:, h], in0=aw[:, h], scalar=dinv_m2[:, h:h + 1],
                                               in1=bc_ps[:, 0:N], op0=ALU.mult, op1=ALU.mult).then_inc(p32_made, 1)
            dve.wait_ge(phi_made, 1)
            nc.vector.tensor_tensor(p_lo[:], p32[:], p_hi[:].bitcast(F32), ALU.subtract).then_inc(plo_made, 1)

            low(4, 0)
            low(4, 1)
            for h in range(NH):
                b_high(1, 3, h)
                b_low(1, 3, h)
            low(5, 0)
            low(5, 1)
            b_step(2, 2)
            for h in range(NH):
                b_low(2, 2, h)
            low(6, 0)
            low(6, 1)
            b_step(3, 1, between=lambda: b2_less_bias(0))
            for h in range(NH):
                b_low(3, 1, h)
            b2_less_bias(1)
            def graph_part(h):
                dve.wait_ge(y_done, NH * (K - 1) + h + 1)
                dve.wait_ge(b2c_made, h + 1)
                nc.vector.tensor_tensor(act_out[:, h], z_ps[0][h][:], b32[0][:, h],
                                        ALU.subtract).then_inc(g_made, 1)

            def leaky_relu(h):
                dve.wait_ge(g_made, h + 1)
                nc.vector.scalar_tensor_tensor(out=leaky[:, h], in0=act_out[:, h], scalar=0.01,
                                               in1=act_out[:, h], op0=ALU.mult, op1=ALU.max).then_inc(leaky_made, 1)

            dve.wait_ge(lin_done, 1)
            dve.wait_ge(x1b_made, 1)
            nc.vector.tensor_tensor(xl[:, 0], lin_ps[0][:], x1[:, 0], ALU.add).then_inc(xl_made, 1)
            graph_part(0)
            leaky_relu(0)
            graph_part(1)
            leaky_relu(1)
            dve.wait_ge(leaky_made, 1)
            dve.wait_ge(xl_made, 1)
            nc.vector.tensor_tensor(res[:, 0], leaky[:, 0], xl[:, 0], ALU.add).then_inc(res_made, 1)
            dve.wait_ge(leaky_made, 2)
            dve.wait_ge(x1b_made, 2)
            for h, span in OUT_PARTS[1:]:
                nc.vector.tensor_tensor(xl[:, h, span], leaky[:, h, span], x1[:, h, span], ALU.add).then_inc(xl_made, 1)
            dve.wait_ge(lin_done, 2)
            for n, (h, span) in enumerate(OUT_PARTS[1:]):
                dve.wait_ge(xl_made, n + 2)
                nc.vector.tensor_tensor(res[:, h, span], lin_ps[h][:, span], xl[:, h, span], ALU.add).then_inc(res_made, 1)

        @block.tensor
        def _(pe):
            def count_chunk(c, first, last):
                for q in range(NH):
                    mm = nc.tensor.matmul(count_ps[q][:, 0:N], onehot[:, c, 1, q * P:(q + 1) * P],
                                          onehot[:, c, 0], start=first, stop=last)
                return mm

            def count_group(g, first=False, last=False):
                for j in range(GRP):
                    pe.wait_ge(onehots, g * GRP + j + 1)
                    mm = count_chunk(g * GRP + j, first and j == 0, last and j == GRP - 1)
                return mm

            pe.wait_ge(warm_made, 1)
            for _ in range(WARM_MATMULS):
                nc.tensor.matmul(aw_ps[0][:, 0:N], warm[:, 0:P], warm[:], start=True, stop=True)
            count_group(0, first=True)
            pe.wait_ge(eye_made, 1)
            for h in range(NH):
                pe.wait_ge(u_made, h + 1)
                for c in range(DC):
                    mm = nc.tensor.transpose(t_ps[c // 2][:, (c % 2) * N + h * P:(c % 2) * N + (h + 1) * P],
                                             u[:, h, c * P:(c + 1) * P], eye[:, P:2 * P])
                mm.then_inc(turned, 1)
            for g in range(1, NG - 1):
                count_group(g)

            def low_wait(s):
                pe.wait_ge(wlo_made, PIECE * (s + 1))

            def times_weight(ps, s, h, terms, first, last):
                slot = W_SLOT[s]
                for n, (a, w) in enumerate(terms):
                    for c in range(DC):
                        if s == 1 and (a, w, h) == (0, 0, 0):
                            if c < DC // 2:
                                pe.wait_ge(xhi_made_act, c + 1)
                            else:
                                pe.wait_ge(xhi_made, 1)
                        mm = nc.tensor.matmul(ps[h][:], (t_hi, t_lo)[a][:, c, h * P:(h + 1) * P],
                                              (w_hi, w_lo)[w][slot][:, c],
                                              start=first and n == 0 and c == 0,
                                              stop=last and n == len(terms) - 1 and c == DC - 1)
                return mm

            pe.wait_ge(thi_made, 2)
            pe.wait_ge(whi_made, PIECE)
            times_weight(sup_ps, 0, 0, [(0, 0)], True, False)
            count_group(NG - 1, last=True).then_inc(counted, 1)
            times_weight(sup_ps, 0, 1, [(0, 0)], True, False)
            pe.wait_ge(tlo_made, 2)
            times_weight(sup_ps, 0, 0, [(1, 0)], False, False)
            pe.wait_ge(adj_made, NH)
            pe.wait_ge(onesr_made, 1)
            for h in range(NH):
                for q in range(NH):
                    mm = nc.tensor.matmul(deg_ps[:, 2 * h:2 * h + 2], adj[:, q, h * P:(h + 1) * P], ones_r[:],
                                          start=q == 0, stop=q == NH - 1)
            mm.then_inc(deg_done, 1)
            times_weight(sup_ps, 0, 1, [(1, 0)], False, False)
            low_wait(0)
            for h in range(NH):
                times_weight(sup_ps, 0, h, [(0, 1)], False, True).then_inc(sup_done, 1)

            def weighted(first, count):
                for c in range(first, first + count):
                    pe.wait_ge(srcs, c + 1)
                    pe.wait_ge(wdst_hi, c + 1)
                    if c in LOW_BY_ACT:
                        pe.wait_ge(wdst_lo_act, LOW_BY_ACT.index(c) + 1)
                    else:
                        pe.wait_ge(wdst_lo, c + 1 - sum(a < c for a in LOW_BY_ACT))
                    for m in range(NH):
                        mm = nc.tensor.matmul(aw_ps[m][:], src_r[:, (c // GRP) % 2, c % GRP, m * P:(m + 1) * P],
                                              wdst_r[:, c].rearrange("p t n -> p (t n)"),
                                              start=c == 0, stop=c == EC - 1)
                        if c == EC - 1:
                            mm.then_inc(aw_done, 1)
                if c % GRP == GRP - 1 and c < EC - 1:
                    mm.then_inc(srcs_used, 1)

            pe.wait_ge(deg_copied, 1)
            for h in range(NH):
                for part, made, tile in ((0, suphi_made, sup_hi), (1, suplo_made, sup_lo)):
                    for q in range(NH):
                        pe.wait_ge(made, q + 1)
                        mm = nc.tensor.matmul(agg_ps[h][:], adj[:, q, h * P:(h + 1) * P], tile[:, q],
                                              start=part == 0 and q == 0, stop=part == 1 and q == NH - 1)
                mm.then_inc(agg_done, 1)

            weighted(0, 8)

            for h in range(NH):
                pe.wait_ge(xn_made, h + 1)
                pe.wait_ge(tlo_made, 2)
                for c in range(DC):
                    mm = nc.tensor.transpose(t_ps[c // 2][:, (c % 2) * N + h * P:(c % 2) * N + (h + 1) * P],
                                             u[:, h, c * P:(c + 1) * P], eye[:, P:2 * P])
                mm.then_inc(xturned, 1)

            weighted(8, 4)

            def z_first(s, ps):
                pe.wait_ge(whi_made, PIECE * (s + 1))
                for h in range(NH):
                    times_weight(ps, s, h, [(0, 0)], True, False)

            def z_second(s, ps):
                pe.wait_ge(xlo_made, 2)
                for h in range(NH):
                    times_weight(ps, s, h, [(1, 0)], False, False)

            def z_high(s, ps):
                z_first(s, ps)
                z_second(s, ps)

            def z_low(s, ps, done=None):
                low_wait(s)
                for h in range(NH):
                    mm = times_weight(ps, s, h, [(0, 1)], False, done is not None)
                    if done is not None:
                        mm.then_inc(done, 1)
                if done is None:
                    mm.then_inc(z_done, 1)

            def linear(h):
                pe.wait_ge(whi_made, PIECE * (LIN + 1))
                low_wait(LIN)
                times_weight(lin_ps, LIN, h, [(0, 0), (1, 0), (0, 1)], True, True).then_inc(lin_done, 1)

            def propagate(i, k):
                hi, lo = b_hi[(i - 1) % 2], b_lo[(i - 1) % 2]
                for h in range(NH):
                    for n, (pt, bt, made) in enumerate(((p_hi, hi, bhi_made), (p_lo, hi, bhi_made),
                                                        (p_hi, lo, blo_made))):
                        for m in range(NH):
                            pe.wait_ge(made, NH * (i - 1) + m + 1)
                            mm = nc.tensor.matmul(z_ps[k][h][:], pt[:, m, h * P:(h + 1) * P], bt[:, m],
                                                  start=False, stop=n == 2 and m == NH - 1)
                    mm.then_inc(y_done, 1)

            def spread_dinv():
                pe.wait_ge(ones_made, 1)
                pe.wait_ge(diag_made, NH)
                pe.wait_ge(b32_made, NH)
                nc.tensor.matmul(bc_ps[:, 0:N], ones[:], diag[:].rearrange("p h n -> p (h n)"), start=True,
                                 stop=True).then_inc(bc_done, 1)

            pe.wait_ge(x1_made, NH)
            z_high(1, z_ps[4])
            weighted(12, 4)
            z_low(1, z_ps[4], y_done)
            z_high(2, z_ps[3])
            z_low(2, z_ps[3])
            weighted(16, 4)
            weighted(20, 12)
            z_high(3, z_ps[2])
            spread_dinv()
            z_low(3, z_ps[2])
            pe.wait_ge(aw_made, NH)
            z_high(4, z_ps[1])
            pe.wait_ge(phi_made, 1)
            pe.wait_ge(plo_made, 1)
            propagate(1, 3)
            z_low(4, z_ps[1])
            z_first(5, z_ps[0])
            propagate(2, 2)
            z_second(5, z_ps[0])
            z_low(5, z_ps[0])
            propagate(3, 1)
            pe.wait_ge(b32_made, NH * 2)
            linear(0)
            propagate(4, 0)
            linear(1)


def kernel(x, src, dst, edge_weight, L0_gnn_weight, L0_gnn_bias, L1_gnn_ln_gamma, L1_gnn_ln_beta,
           L1_gnn_cheb_W, L1_gnn_cheb_b, L1_gnn_lin_W, L1_gnn_lin_b):
    import concourse.bacc as bacc
    from concourse.bass_utils import run_bass_kernel_spmd

    a = {k: np.asarray(v) for k, v in locals().items() if k not in ("bacc", "run_bass_kernel_spmd")}
    cheb = a["L1_gnn_cheb_W"]
    arrays = {
        "x": a["x"],
        "edges": np.stack([a["src"].reshape(P, EC), a["dst"].reshape(P, EC)], axis=2),
        "edge_w": a["edge_weight"].reshape(P, EC),
        "w0": a["L0_gnn_weight"],
        "wt": np.stack([cheb[k].T for k in range(K - 1, -1, -1)] + [a["L1_gnn_lin_W"].T]),
        "cols": np.stack([a[n].reshape(DC, P).T for n in ("L1_gnn_ln_gamma", "L1_gnn_ln_beta")], axis=1),
        "rows": np.broadcast_to(np.stack([a["L0_gnn_bias"], a["L1_gnn_cheb_b"], a["L1_gnn_lin_b"]]), (P, 3, D)),
    }
    arrays = {n: np.ascontiguousarray(v) for n, v in arrays.items()}
    nc = bacc.Bacc("TRN2", target_bir_lowering=False, num_devices=1)
    aps = [nc.dram_tensor(n, v.shape, mybir.dt.from_np(v.dtype), kind="ExternalInput").ap()
           for n, v in arrays.items()]
    aps.append(nc.dram_tensor("out", (N, D), F32, kind="ExternalOutput").ap())
    build(nc, *aps)
    return run_bass_kernel_spmd(nc, [arrays], core_ids=[0]).results[0]["out"]
```
